# Optimizing a Trainium2 kernel written in Bass

```python
import numpy as np
import jax
import jax.numpy as jnp

def _softmax(x, axis=-1):
    return jax.nn.softmax(x, axis=axis)

def _gelu(x):
    return jax.nn.gelu(x, approximate=True)

def _silu(x):
    return jax.nn.silu(x)

def _sigmoid(x):
    return jax.nn.sigmoid(x)

def _layernorm(x, axis=-1, eps=1e-05):
    m = jnp.mean(x, axis=axis, keepdims=True)
    v = jnp.var(x, axis=axis, keepdims=True)
    return (x - m) / jnp.sqrt(v + eps)

def _scatter_add(tgt, idx, src, axis=0):
    return tgt.at[idx].add(src)

def _segment_sum(src, seg, n):
    return jax.ops.segment_sum(src, seg, n)
kernel_name = 'mk_adj_preln_d2_adj_r2_3ff606'

def setup_inputs(seed: int=0):
    np.random.seed(seed)
    _w = jnp.asarray

    def _rec_inputs():
        import jax
        import jax.numpy as jnp
        _gk = jax.random.key(seed)
        x = -0.0002928 + 1 * jax.random.normal(jax.random.fold_in(_gk, 1), (4096, 128), jnp.float32)
        _w = (1.0 + jnp.arange(4096, dtype=jnp.float32)) ** (-0.5)
        _w = _w / _w.mean()
        _pij = jnp.clip(0.000488281 * _w[:, None] * _w[None, :], 0.0, 1.0)
        _a = jax.random.uniform(jax.random.fold_in(_gk, 2), (4096, 4096)) < _pij
        _a = jnp.logical_or(_a, jnp.eye(4096, dtype=bool))
        _af = _a.astype(jnp.float32)
        _af = _af * jax.random.uniform(jax.random.fold_in(_gk, 3), (4096, 4096), jnp.float32, 0.05, 1)
        adj = _af
        return (x, adj)
    x, adj = _rec_inputs()

    def _L0_gnn_setup():
        import jax, jax.numpy as jnp
        import numpy as np
        N, D_IN, D_OUT = (8192, 128, 128)
        key = jax.random.key(seed)
        k1, k2, k3, k4 = jax.random.split(key, 4)
        x = jax.random.normal(k1, (N, D_IN), dtype=jnp.float32)
        adj = jax.random.uniform(k2, (N, N), dtype=jnp.float32)
        W = jax.random.normal(k3, (D_IN, D_OUT), dtype=jnp.float32) / np.sqrt(D_IN)
        b = jax.random.normal(k4, (D_OUT,), dtype=jnp.float32) * 0.01
        return {'x': x, 'adj': adj, 'W': W, 'b': b}
    _L0_gnn_all = _L0_gnn_setup()
    _L0_gnn_in = {k: v for k, v in _L0_gnn_all.items() if k in ('W', 'b')}
    del _L0_gnn_all

    def _L1_gnn_setup():
        import jax, jax.numpy as jnp
        import numpy as np
        N, H, HEADS = (2048, 128, 3)
        ALPHA = 0.2
        NEG_INF = -9000000000000000.0

        def _sign_adj(key, n, density):
            k1, k2 = jax.random.split(key)
            mask = jax.random.uniform(k1, (n, n)) < density
            sign = jnp.where(jax.random.uniform(k2, (n, n)) < 0.5, -1.0, 1.0)
            adj = jnp.where(mask, sign, 0.0).astype(jnp.float32)
            idx = jnp.arange(n)
            return adj.at[idx, idx].set(1.0)

        def _gru_cell(x, hstate, Wih, Whh, bih, bhh):
            gi = x @ Wih.T + bih
            gh = hstate @ Whh.T + bhh
            ir, iz, inn = jnp.split(gi, 3, axis=1)
            hr, hz, hn = jnp.split(gh, 3, axis=1)
            r = jax.nn.sigmoid(ir + hr)
            z = jax.nn.sigmoid(iz + hz)
            n = jnp.tanh(inn + r * hn)
            return (1.0 - z) * n + z * hstate

        def _gat_head(h, node_adj, edge_adj, W, a):
            hW = h @ W
            hp = (node_adj > 0).astype(hW.dtype) @ hW
            hm = (node_adj < 0).astype(hW.dtype) @ hW
            e_plus = jax.nn.leaky_relu(jnp.concatenate([hp, hm], axis=1) @ a, ALPHA)[:, 0]
            e_minus = jax.nn.leaky_relu(jnp.concatenate([hm, hp], axis=1) @ a, ALPHA)[:, 0]
            att = jnp.where(edge_adj > 0, e_plus[None, :], NEG_INF)
            att = jnp.where(edge_adj < 0, e_minus[None, :], att)
            att = jax.nn.softmax(att, axis=1)
            return att * edge_adj @ hW
        key = jax.random.key(seed)
        ks = jax.random.split(key, 16)
        std = 0.01
        gain = 1.414
        return {'h': jax.random.normal(ks[0], (N, H), jnp.float32), 'node_adj': _sign_adj(ks[1], N, 0.005), 'edge_adj': _sign_adj(ks[2], N, 0.005), 'gat_W': jax.random.normal(ks[3], (HEADS, H, H), jnp.float32) * (gain / np.sqrt(H, dtype=np.float32)), 'gat_a': jax.random.normal(ks[4], (HEADS, 2 * H, 1), jnp.float32) * 0.1, 'edge_Wih': jax.random.normal(ks[5], (3 * H, H), jnp.float32) * std, 'edge_Whh': jax.random.normal(ks[6], (3 * H, H), jnp.float32) * std, 'edge_bih': jnp.zeros((3 * H,), jnp.float32), 'edge_bhh': jnp.zeros((3 * H,), jnp.float32), 'node_Wih': jax.random.normal(ks[7], (3 * H, H), jnp.float32) * std, 'node_Whh': jax.random.normal(ks[8], (3 * H, H), jnp.float32) * std, 'node_bih': jnp.zeros((3 * H,), jnp.float32), 'node_bhh': jnp.zeros((3 * H,), jnp.float32)}
    _L1_gnn_all = _L1_gnn_setup()
    _L1_gnn_in = {k: v for k, v in _L1_gnn_all.items() if k in ('gat_W', 'gat_a', 'edge_Wih', 'edge_Whh', 'edge_bih', 'edge_bhh', 'node_Wih', 'node_Whh', 'node_bih', 'node_bhh')}
    del _L1_gnn_all
    return {'x': x, 'adj': adj, 'L0_gnn_W': _L0_gnn_in['W'], 'L0_gnn_b': _L0_gnn_in['b'], 'L1_gnn_gat_W': _L1_gnn_in['gat_W'], 'L1_gnn_gat_a': _L1_gnn_in['gat_a'], 'L1_gnn_edge_Wih': _L1_gnn_in['edge_Wih'], 'L1_gnn_edge_Whh': _L1_gnn_in['edge_Whh'], 'L1_gnn_edge_bih': _L1_gnn_in['edge_bih'], 'L1_gnn_edge_bhh': _L1_gnn_in['edge_bhh'], 'L1_gnn_node_Wih': _L1_gnn_in['node_Wih'], 'L1_gnn_node_Whh': _L1_gnn_in['node_Whh'], 'L1_gnn_node_bih': _L1_gnn_in['node_bih'], 'L1_gnn_node_bhh': _L1_gnn_in['node_bhh']}

def reference(x, adj, L0_gnn_W, L0_gnn_b, L1_gnn_gat_W, L1_gnn_gat_a, L1_gnn_edge_Wih, L1_gnn_edge_Whh, L1_gnn_edge_bih, L1_gnn_edge_bhh, L1_gnn_node_Wih, L1_gnn_node_Whh, L1_gnn_node_bih, L1_gnn_node_bhh):
    import jax
    import jax.numpy as jnp

    def _L0_gnn_ref(x, adj, W, b):
        import jax, jax.numpy as jnp
        import numpy as np
        N, D_IN, D_OUT = (8192, 128, 128)
        support = jnp.matmul(x, W)
        out = jnp.matmul(adj, support) + b
        return jax.nn.relu(out)

    def _L1_gnn_ref(h, node_adj, edge_adj, gat_W, gat_a, edge_Wih, edge_Whh, edge_bih, edge_bhh, node_Wih, node_Whh, node_bih, node_bhh):
        import jax, jax.numpy as jnp
        import numpy as np
        N, H, HEADS = (2048, 128, 3)
        ALPHA = 0.2
        NEG_INF = -9000000000000000.0

        def _sign_adj(key, n, density):
            k1, k2 = jax.random.split(key)
            mask = jax.random.uniform(k1, (n, n)) < density
            sign = jnp.where(jax.random.uniform(k2, (n, n)) < 0.5, -1.0, 1.0)
            adj = jnp.where(mask, sign, 0.0).astype(jnp.float32)
            idx = jnp.arange(n)
            return adj.at[idx, idx].set(1.0)

        def _gru_cell(x, hstate, Wih, Whh, bih, bhh):
            gi = x @ Wih.T + bih
            gh = hstate @ Whh.T + bhh
            ir, iz, inn = jnp.split(gi, 3, axis=1)
            hr, hz, hn = jnp.split(gh, 3, axis=1)
            r = jax.nn.sigmoid(ir + hr)
            z = jax.nn.sigmoid(iz + hz)
            n = jnp.tanh(inn + r * hn)
            return (1.0 - z) * n + z * hstate

        def _gat_head(h, node_adj, edge_adj, W, a):
            hW = h @ W
            hp = (node_adj > 0).astype(hW.dtype) @ hW
            hm = (node_adj < 0).astype(hW.dtype) @ hW
            e_plus = jax.nn.leaky_relu(jnp.concatenate([hp, hm], axis=1) @ a, ALPHA)[:, 0]
            e_minus = jax.nn.leaky_relu(jnp.concatenate([hm, hp], axis=1) @ a, ALPHA)[:, 0]
            att = jnp.where(edge_adj > 0, e_plus[None, :], NEG_INF)
            att = jnp.where(edge_adj < 0, e_minus[None, :], att)
            att = jax.nn.softmax(att, axis=1)
            return att * edge_adj @ hW
        dn = jnp.diag(node_adj)
        de = jnp.diag(edge_adj)
        idx = jnp.arange(node_adj.shape[0])
        node_adj_norm = node_adj.at[idx, idx].add(-dn)
        edge_adj_norm = edge_adj.at[idx, idx].add(-de)
        node_support = node_adj_norm @ h
        edge_output = _gru_cell(node_support, h, edge_Wih, edge_Whh, edge_bih, edge_bhh)
        edge_support = _gat_head(h, node_adj_norm, edge_adj_norm, gat_W[0], gat_a[0])
        for i in range(1, HEADS):
            edge_support = edge_support + _gat_head(h, node_adj_norm, edge_adj_norm, gat_W[i], gat_a[i])
        edge_support = edge_support / HEADS
        node_output = _gru_cell(edge_support, h, node_Wih, node_Whh, node_bih, node_bhh)
        return de[:, None] * edge_output + dn[:, None] * node_output
    h = jnp.maximum(_layernorm(x, axis=-1), 0.0)
    x = x + _L0_gnn_ref(h, adj, L0_gnn_W, L0_gnn_b)
    h = jnp.maximum(_layernorm(x, axis=-1), 0.0)
    x = x + _L1_gnn_ref(h, adj, adj, L1_gnn_gat_W, L1_gnn_gat_a, L1_gnn_edge_Wih, L1_gnn_edge_Whh, L1_gnn_edge_bih, L1_gnn_edge_bhh, L1_gnn_node_Wih, L1_gnn_node_Whh, L1_gnn_node_bih, L1_gnn_node_bhh)
    return x

_drawn_inputs = setup_inputs


def setup_inputs(seed=0):
    import zlib

    import numpy as np

    out = dict(_drawn_inputs(seed))
    spreads = {'L1_gnn_edge_bih': (0.0, 0.401),
     'L1_gnn_edge_bhh': (0.0, 0.788),
     'L1_gnn_node_bih': (0.0, 0.397),
     'L1_gnn_node_bhh': (0.0, 0.671)}
    factors = {'L0_gnn_b': 8.0,
     'L1_gnn_gat_W': 8.0,
     'L1_gnn_gat_a': 8.0,
     'L1_gnn_edge_Wih': 3.137,
     'L1_gnn_edge_Whh': 6.045,
     'L1_gnn_node_Wih': 8.0,
     'L1_gnn_node_Whh': 5.888}
    for name, (base, spread) in spreads.items():
        noise = np.random.default_rng([zlib.crc32(name.encode()), seed]).standard_normal(out[name].shape)
        drawn = base * np.exp(spread * noise) if base else spread * noise
        out[name] = jnp.asarray(drawn.astype(out[name].dtype))
    for name, factor in factors.items():
        out[name] = (out[name] * factor).astype(out[name].dtype)
    return out
```

```python
from contextlib import ExitStack

import concourse.bass as bass
from concourse import mybir
from concourse.bass import ds

F32 = mybir.dt.float32
BF16 = mybir.dt.bfloat16
FP8 = mybir.dt.float8e4
U8 = mybir.dt.uint8
U32 = mybir.dt.uint32
I32 = mybir.dt.int32
ALU = mybir.AluOpType
ACT = mybir.ActivationFunctionType
AX = mybir.AxisListType

P = 128
N = 4096
NT = N // P
CH = 512
NC = N // CH
QT = CH // P
HEADS = 3
EPS = 1e-5
ALPHA = 0.2

GRP1 = 2
NG1 = NT // GRP1
RING1 = 4
GRP = 4
NG = NT // GRP
RING = 4

CODE_STEP, CODE_ZERO = 80.0, 128.0
POS_CODE, NEG_CODE = CODE_ZERO + CODE_STEP, CODE_ZERO - CODE_STEP
POS_BITS, POS_VALUE = 0x40404040, 2.0
NEG_BITS, NEG_VALUE = 0x20202020, 0.125

WIN = 8
WIDTH = 140
KG = HEADS * WIN
RMAX = bass.bass_isa.ReduceOp.max
LN2 = 0.6931471805599453
HUGE = 1e30
COARSE = 1e6
CAP = 80.0

WIDE_OWN = 2 + NT * (2 + 2 * HEADS) + 1 + NT * 2 * HEADS * 2 + HEADS
SIGNED_OWN = NG + NT * HEADS
OWN4 = 6
OWN1 = 1 + 2 * QT + 5 + QT


class Chain:

    def __init__(self, eng, sem, idle):
        self.eng, self.sem, self.idle, self.at = eng, sem, idle, 0

    def stand(self):
        self.eng.sem_inc(self.idle, 1)

    def step(self, ins, wait=True):
        ins.then_inc(self.sem, 1)
        self.at = self.at + 1
        if wait:
            self.eng.wait_ge(self.sem, self.at)


def build(nc, ins, out):
    ctx = ExitStack()
    with ctx:
        def sb(name, shape, dt):
            return ctx.enter_context(nc.sbuf_tensor(name, shape, dt))

        def sem(name):
            return ctx.enter_context(nc.semaphore(name))

        h_dram = nc.dram_tensor("h_scratch", (NC, P, QT * P), F32)
        hT_dram = nc.dram_tensor("hT_scratch", (NC, P, CH), F32)
        guard_dram = nc.dram_tensor("guard_scratch", (HEADS, N), F32)
        rden_dram = nc.dram_tensor("rden_scratch", (HEADS, N), F32)

        big = sb("big", [P, NT * N], U8)
        code32 = big[:, :].bitcast(U32).rearrange("p (t j) -> p t j", t=NT)
        x1 = sb("x1", [P, NT, P], F32)
        S = sb("S", [P, NT, P], F32)
        ring1 = sb("ring1", [P, RING1, GRP1, CH], F32)
        small = sb("small", [P, 1280], F32)
        vecs = sb("vecs", [P, NT * 25], F32)
        ident = sb("ident", [P, P], F32)
        notI = sb("notI", [P, P], U8)
        w0 = sb("w0", [P, P], F32)
        b0 = sb("b0", [P, 1], F32)
        wT = sb("wT", [P, HEADS, P], F32)
        av = sb("av", [P, 2 * HEADS], F32)
        V = sb("V", [P, 2 * HEADS], F32)
        gx = sb("gx", [P, QT * 2, P], F32)
        gT = sb("gT", [P, 2, CH], F32)
        oT = sb("oT", [P, CH], F32)
        sgn = sb("sgn", [P, 2, GRP1 * CH], BF16)

        wsum = sb("wsum", [P, NT, KG], F32)
        tops = sb("tops", [P, 96], F32)
        rows = sb("rows", [HEADS * NT, 2, P], F32)
        masks = S[:, :, :].bitcast(FP8).rearrange("p t (a s r j) -> p (t a s r j)", a=1, s=1, r=1)\
            .rearrange("p (b s t j) -> p b s t j", b=2, s=2, t=NT)
        masks32 = S[:, :, :].bitcast(U32).rearrange("p t j -> p (t j)").rearrange("p (b s t j) -> p b s t j", b=2, s=2, t=NT)
        r1 = ring1[:, :, :, :].rearrange("p a b c -> p (a b c)")
        mvW = r1[:, 0:2 * NT * KG * 3 // 2].bitcast(BF16).rearrange("p (s t c) -> p s t c", s=2, t=NT)
        tt = r1[:, 2304:2304 + NT * KG]
        mm = r1[:, 3072:3072 + NT * KG]
        ww = gx[:, :, :].rearrange("p a b -> p (a b)")[:, 0:NT * KG]
        mvU = sb("mvU", [P, 2, NT, 21], BF16)

        place = [0]

        def over(shape, dt=F32, size=4):
            n = 1
            for d in shape:
                n *= d
            a = big[:, place[0]:place[0] + n * size].bitcast(dt)
            place[0] += n * size
            names = " ".join(f"d{i}" for i in range(len(shape)))
            return a if len(shape) == 1 else a.rearrange(f"p ({names}) -> p {names}", **{f"d{i}": d for i, d in enumerate(shape)})

        a4 = over((RING, GRP, CH))
        args = over((2, HEADS, CH))
        expo = over((2, HEADS, CH))
        wgt = over((RING, HEADS, CH))
        isneg = over((GRP * CH,), BF16, 2)
        ngB = over((2 * HEADS, CH))
        rdB = over((2 * HEADS, CH))
        h = over((NT, P))
        assert place[0] <= NT * N
        slots = [S[:, 4 * i:4 * i + 4, :].rearrange("p t j -> p (t j)") for i in range(8)] + \
                [ring1[:, i // 2, i % 2, :] for i in range(8)]
        nn, sup, es, hTc = slots[0:3], slots[3], slots[4], slots[5]
        gate_r, gate_z, cand, mix, y_edge, ot = slots[6], slots[7], slots[8], slots[9], slots[10], slots[11]
        cell_n = slots[12]
        wih = gT[:, :, :].rearrange("p a b -> p (a b)")[:, 0:2 * 3 * P].rearrange("p (c g d) -> p c g d", c=2, g=3)
        whh = sgn[:, :, :].rearrange("p a b -> p (a b)").bitcast(F32)[:, 0:2 * 3 * P]\
            .rearrange("p (c g d) -> p c g d", c=2, g=3)
        gatw = oT[:, 0:HEADS * P].rearrange("p (k d) -> p k d", k=HEADS)
        offdiag = small[:, 0:(2 * NC - 1) * P // 2].bitcast(BF16)
        bias = small[:, 1000:1012]
        hbias = small[:, 1012:1016]
        dg = small[:, 1016:1016 + NT]

        s_flat = S[:, :, :].rearrange("p t j -> p (t j)")
        wide_acc = s_flat[:, 0:HEADS * CH]
        wide_ng = s_flat[:, HEADS * CH:2 * HEADS * CH]
        not_pos, not_neg = s_flat[:, 3072:3072 + CH], s_flat[:, 3072 + CH:3072 + 2 * CH]
        wide_args, wide_expo = r1[:, 0:HEADS * CH], r1[:, HEADS * CH:2 * HEADS * CH]
        all_ones = r1[:, 2 * HEADS * CH:2 * HEADS * CH + P]
        is_wide, is_signed = tops[0:1, 72:73].bitcast(I32), tops[0:1, 73:74].bitcast(I32)

        stats = small[:, 0:NT * 6].rearrange("p (t s) -> p t s", t=NT)
        mv = small[:, 192:192 + NT * 2].rearrange("p (t s) -> p t s", t=NT)
        sd = small[:, 256:288]
        sq = small[:, 288:320]
        rstd = small[:, 320:352]
        u6 = vecs[:, 0:NT * 6].rearrange("p (t s) -> p t s", t=NT)
        scores = vecs[:, NT * 6:NT * 13].rearrange("p (t s) -> p t s", t=NT)
        delta = vecs[:, NT * 13:NT * 16].rearrange("p (t s) -> p t s", t=NT)
        guard = vecs[:, NT * 16:NT * 19]
        rden = vecs[:, NT * 19:NT * 22]
        caps = guard.rearrange("p (t k) -> p t k", t=NT)
        nguard = vecs[:, NT * 22:NT * 25]

        bank = [ctx.enter_context(nc.psum_tensor(f"bank{i}", [P, CH], F32)) for i in range(8)]

        xin_done = [sem(f"xin_done{i}") for i in range(2)]
        consts_in = sem("consts_in")
        const_ready = sem("const_ready")
        v_done = sem("v_done")
        v_ready = sem("v_ready")
        dve_own = sem("dve_own")
        dve_idle, pe_idle, pool_idle = sem("dve_idle"), sem("pe_idle"), sem("pool_idle")
        var_ready = sem("var_ready")
        sqrt_ready = sem("sqrt_ready")
        g0_ready = sem("g0_ready")
        g0T_done = sem("g0T_done")
        g0T_ready = sem("g0T_ready")
        S_done = sem("S_done")
        S_ready = sem("S_ready")
        a1_in = [sem(f"a1_in{i}") for i in range(RING1)]
        a1_used_pe = sem("a1_used_pe")
        a1_used_act = sem("a1_used_act")
        sgn_ready = sem("sgn_ready")
        code_ready = sem("code_ready")
        oT_ready = sem("oT_ready")
        o_nat = sem("o_nat")
        h_ready = sem("h_ready")
        h_stored = sem("h_stored")
        hT_done = sem("hT_done")
        hT_ready = sem("hT_ready")
        hT_stored = sem("hT_stored")
        u_done = sem("u_done")
        u_ready = sem("u_ready")
        diag_ready = sem("diag_ready")
        mv_ready = sem("mv_ready")
        mask_ready = sem("mask_ready")
        mask_used = sem("mask_used")
        sums_taken = sem("sums_taken")
        S_free = sem("S_free")
        late_in = sem("late_in")
        a4_clean = sem("a4_clean")
        tile_done = sem("tile_done")
        arg4_ready = sem("arg4_ready")
        e_ready = sem("e_ready")
        w_ready = sem("w_ready")
        guard_stored = sem("guard_stored")
        h_in = sem("h_in")
        hT_in = sem("hT_in")
        sup_taken = sem("sup_taken")
        nn_taken = sem("nn_taken")
        es_done = sem("es_done")
        es_ready = sem("es_ready")
        gate_done = sem("gate_done")
        ni_done = sem("ni_done")
        act_gate = sem("act_gate")
        pre_ready = sem("pre_ready")
        cand_ready = sem("cand_ready")
        diff_ready = sem("diff_ready")
        y_ready = sem("y_ready")
        ysum_ready = sem("ysum_ready")
        yT_done = sem("yT_done")
        ot_ready = sem("ot_ready")
        out_stored = sem("out_stored")
        dve4 = sem("dve4")
        hb_ready = sem("hb_ready")
        offd_ready = sem("offd_ready")
        a4_in = [sem(f"a4_in{i}") for i in range(RING)]
        gd_in = [sem(f"gd_in{i}") for i in range(2)]
        ext_ready = sem("ext_ready")
        all_ext = sem("all_ext")
        arg_ready = sem("arg_ready")
        exp_ready = sem("exp_ready")
        nat_ready = sem("nat_ready")
        rows_done = sem("rows_done")
        rows_ready = sem("rows_ready")
        pool_own = sem("pool_own")
        xdg_in = sem("xdg_in")
        sp_idle, act_idle = sem("sp_idle"), sem("act_idle")
        flags_ready = sem("flags_ready")
        wide_own = sem("wide_own")
        wide_max = sem("wide_max")
        wide_reduced = sem("wide_reduced")
        wide_arg = sem("wide_arg")
        wide_exp = sem("wide_exp")
        wide_sum = sem("wide_sum")
        wide_total = sem("wide_total")
        wide_rows = sem("wide_rows")
        wide_stored = sem("wide_stored")
        wide_done = sem("wide_done")
        signed_own = sem("signed_own")

        x_v = ins["x"].rearrange("(t p) d -> p t d", p=P)
        out_v = out.rearrange("(c q p) d -> c p q d", p=P, q=QT)
        aT_v = ins["adjT"]

        block = ctx.enter_context(nc.Block())

        @block.sync
        def _(sp):
            for i in range(2):
                half = slice(i * NT // 2, (i + 1) * NT // 2)
                sp.dma_start(x1[:, half, :], x_v[:, half, :]).then_inc(xin_done[i], 16)
            sp.dma_start(w0[:, :], ins["L0_gnn_W"]).then_inc(consts_in, 16)
            sp.dma_start(b0[:, :], ins["L0_gnn_b"].rearrange("(p o) -> p o", o=1)).then_inc(consts_in, 16)
            sp.dma_start(wT[:, :, :], ins["gat_WT"].rearrange("k e d -> e k d")).then_inc(consts_in, 16)
            sp.dma_start(av[:, :], ins["gat_a"]).then_inc(consts_in, 16)
            sp.dma_start(dg, ins["diag"]).then_inc(xdg_in, 16)

            def load1(jc, g):
                sp.dma_start(ring1[:, g % RING1, :, :], aT_v[jc, :, g * GRP1:(g + 1) * GRP1, :])\
                  .then_inc(a1_in[g % RING1], 16)

            for g in range(RING1):
                load1(0, g)

            def steady(jc, groups):
                for g in range(groups):
                    sp.wait_ge(a1_used_pe, jc * NG1 + (g + 1))
                    sp.wait_ge(a1_used_act, jc * NG1 + (g + 1))
                    ahead = g + RING1
                    if ahead < NG1:
                        sp.dma_start(ring1[:, ahead % RING1, :, :],
                                     aT_v[ds(jc, 1), :, ahead * GRP1:(ahead + 1) * GRP1, :].rearrange("o p t j -> (o p) t j"))\
                          .then_inc(a1_in[ahead % RING1], 16)
                    else:
                        ahead -= NG1
                        sp.dma_start(ring1[:, ahead % RING1, :, :],
                                     aT_v[ds(jc + 1, 1), :, ahead * GRP1:(ahead + 1) * GRP1, :].rearrange("o p t j -> (o p) t j"))\
                          .then_inc(a1_in[ahead % RING1], 16)

            with sp.Fori(0, NC - 1) as jc:
                steady(jc, NG1)
            steady(NC - 1, NG1 - RING1)

            sp.wait_ge(hT_stored, 16 + 16 * NC)
            sp.wait_ge(u_ready, NC)
            sp.wait_ge(code_ready, 2 + NG1 * NC)
            for dst, name in ((wih[:, 0], "edge_WihT"), (wih[:, 1], "node_WihT"), (whh[:, 0], "edge_WhhT"),
                              (whh[:, 1], "node_WhhT"), (gatw, "gat_W"), (bias, "bias")):
                sp.dma_start(dst, ins[name]).then_inc(late_in, 16)
            def load4(c, g, slot):
                src = aT_v[c, :, g * GRP:(g + 1) * GRP, :] if isinstance(c, int) else \
                    aT_v[ds(c, 1), :, g * GRP:(g + 1) * GRP, :].rearrange("o p t j -> (o p) t j")
                sp.dma_start(a4[:, slot, :, :], src).then_inc(a4_in[slot], 16)

            sp.wait_ge(flags_ready, 1)
            wide = sp.value_load(is_wide, min_val=0, max_val=1)
            sp.wait_ge(mask_used, 2 + 2 * NT)
            with sp.If(wide > 0):
                sp.wait_ge(rows_ready, 1)
                sp.wait_ge(wide_done, 1)
                for g in range(RING):
                    load4(0, g, g)
            with sp.Else():
                for g in range(RING):
                    load4(0, g, g)
                sp.wait_ge(rows_ready, 1)
                for s, dst in enumerate((guard_dram, rden_dram)):
                    sp.dma_start(dst[:, :].rearrange("k (t p) -> t k p", p=P), rows[:, s, :]).then_inc(guard_stored, 16)
                sp.wait_ge(guard_stored, 32)

            def load_rows(c, par):
                for src, dst in ((guard_dram, ngB), (rden_dram, rdB)):
                    where = slice(c * CH, (c + 1) * CH) if isinstance(c, int) else ds(c * CH, CH)
                    at = slice(par * HEADS, (par + 1) * HEADS) if isinstance(par, int) else ds(par * HEADS, HEADS)
                    sp.dma_start(dst[:, at, :], src[:, where].partition_broadcast(P)).then_inc(gd_in[0], 16)

            load_rows(0, 0)
            sp.dma_start(h.rearrange("p (c q) d -> p c (q d)", c=NC), h_dram[:, :, :].rearrange("c p j -> p c j")).then_inc(h_in, 16)

            def chunk_loads(c, groups, first=False, last=False):
                for g in groups:
                    if g == 4 and not last:
                        if not first:
                            sp.wait_ge(nn_taken, c * HEADS)
                        load_rows(c + 1, (c + 1) % 2)
                    if g == 6:
                        if not first:
                            sp.wait_ge(yT_done, c)
                        sp.dma_start(hTc, hT_dram[ds(c, 1), :, :].rearrange("o p j -> (o p) j")).then_inc(hT_in, 16)
                    if last and g >= NG - RING:
                        continue
                    sp.wait_ge(tile_done, c * NT + (4 + GRP * (g + 1)))
                    if g + RING < NG:
                        load4(c, g + RING, g % RING)
                    else:
                        load4(c + 1, g + RING - NG, g % RING)

            chunk_loads(0, range(NG), first=True)
            with sp.Fori(1, NC - 1) as c:
                chunk_loads(c, range(NG))
            chunk_loads(NC - 1, range(NG), last=True)

        @block.tensor
        def _(pe):
            pe.wait_ge(consts_in, 64)
            for s in range(2):
                for k in range(HEADS):
                    c = s * HEADS + k
                    last = nc.tensor.matmul(bank[7][:, c:c + 1], wT[:, k, :], av[:, c:c + 1], start=True, stop=True)
            last.then_inc(v_done, 1)
            pe.wait_ge(const_ready, 2)
            with pe.Fori(0, NC // 2) as i:
                for b in range(2):
                    pe.wait_ge(g0_ready, i * 2 + (b + 1))
                    for q in range(QT):
                        last = nc.tensor.transpose(bank[b][:, q * P:(q + 1) * P], gx[:, b * QT + q, :], ident[:, :])
                    last.then_inc(g0T_done, 1)
                for b in range(2):
                    pe.wait_ge(g0T_ready, i * 2 + (b + 1))
                    for q in range(QT):
                        last = nc.tensor.matmul(bank[2 + b][:, q * P:(q + 1) * P], gT[:, b, q * P:(q + 1) * P], w0[:, :],
                                                start=True, stop=True)
                    last.then_inc(S_done, 1)
            pe.wait_ge(S_ready, NC)

            def products(jc, groups):
                for g in groups:
                    pe.wait_ge(a1_in[g % RING1], jc * (16 * NG1 // RING1) + 16 * (g // RING1 + 1))
                    for r in range(GRP1):
                        it = g * GRP1 + r
                        last = nc.tensor.matmul(bank[0][:, :], S[:, it, :], ring1[:, g % RING1, r, :],
                                                start=(it == 0), stop=(it == NT - 1))
                    last.then_inc(a1_used_pe, 1)

            def to_natural(done):
                pe.wait_ge(oT_ready, done)
                for q in range(QT):
                    last = nc.tensor.transpose(bank[1][:, q * P:(q + 1) * P], oT[:, q * P:(q + 1) * P], ident[:, :])
                last.then_inc(o_nat, 1)

            def transpose_h(done):
                pe.wait_ge(h_ready, done)
                for q in range(QT):
                    last = nc.tensor.transpose(bank[2][:, q * P:(q + 1) * P], gx[:, q, :], ident[:, :])
                last.then_inc(hT_done, 1)

            def project(done):
                pe.wait_ge(hT_ready, done)
                for q in range(QT):
                    last = nc.tensor.matmul(bank[3][:, q * 8:q * 8 + 6], gT[:, 0, q * P:(q + 1) * P], V[:, :],
                                            start=True, stop=True)
                last.then_inc(u_done, 1)

            products(0, range(NG1))
            with pe.Fori(1, NC) as jc:
                pe.wait_ge(oT_ready, jc)
                products(jc, range(0, 2))
                to_natural(jc)
                products(jc, range(2, 8))
                transpose_h(jc)
                products(jc, range(8, 12))
                project(jc)
                products(jc, range(12, NG1))
            to_natural(NC)
            transpose_h(NC)
            project(NC)

            def mask_products(moving, cols, turn0):
                with pe.Fori(0, NT // 2) as i:
                    for b in range(2):
                        pe.wait_ge(mask_ready, i * 2 + (turn0 + b + 1))
                        pe.wait_ge(sums_taken, i * 2 + (turn0 + b + 1))
                        pe.sem_inc(pe_idle, 1)
                        for s in range(2):
                            for it in range(NT):
                                last = nc.tensor.matmul(bank[b][:, 0:cols], masks[:, b, s, it, :],
                                                        moving[:, s, it, :], start=(s == 0 and it == 0),
                                                        stop=(s == 1 and it == NT - 1))
                        last.then_inc(mask_used, 1)

            nc.tensor.drain().then_inc(S_free, 1)
            pe.wait_ge(mv_ready, 1)
            mask_products(mvU, 21, 0)
            pe.wait_ge(mv_ready, 2)
            mask_products(mvW, KG * 3, NT)
            pe.wait_ge(nat_ready, 1)
            nc.tensor.transpose(bank[2][0:HEADS * NT, 0:P], nguard, ident[:, :])
            nc.tensor.transpose(bank[2][0:HEADS * NT, P:2 * P], rden, ident[:, :])\
              .then_inc(rows_done, 1)

            pe.wait_ge(flags_ready, 1)
            wide = pe.value_load(is_wide, min_val=0, max_val=1)
            with pe.If(wide > 0):
                with pe.Fori(0, NC) as c:
                    pe.wait_ge(wide_sum, c + 1)
                    for k in range(HEADS):
                        last = nc.tensor.matmul(bank[k][:, :], all_ones, wide_acc[:, k * CH:(k + 1) * CH],
                                                start=True, stop=True)
                    last.then_inc(wide_total, 1)
            with pe.Else():
                pe.sem_inc(pe_idle, 1)

            def tile(c, it):
                g, r = it // GRP, it % GRP
                if r == 0:
                    pe.wait_ge(a4_clean, c * NG + (g + 1))
                if it == 0 and not (isinstance(c, int) and c == 0):
                    pe.wait_ge(sup_taken, c)
                nc.tensor.matmul(bank[3][:, :], h[:, it, :], a4[:, g % RING, r, :], start=(it == 0), stop=(it == NT - 1))
                for k in range(HEADS):
                    pe.wait_ge(w_ready, c * (NT * HEADS) + (6 + it * HEADS + k + 1))
                    if it == 0 and not (isinstance(c, int) and c == 0):
                        pe.wait_ge(nn_taken, c * HEADS + (k + 1 - HEADS))
                    last = nc.tensor.matmul(bank[k][:, :], h[:, it, :], wgt[:, it % RING, k, :],
                                            start=(it == 0), stop=(it == NT - 1))
                last.then_inc(tile_done, 1)

            def hidden(cell):
                for b, gate in ((5, 0), (6, 1), (4, 2)):
                    last = nc.tensor.matmul(bank[b][:, :], whh[:, cell, gate, :], hTc, start=True, stop=(b == 4))
                return last

            def after(e, it):
                if it == "start":
                    pe.wait_ge(hT_in, e * 16)
                    hidden(0)
                if it == 1:
                    pe.wait_ge(nn_taken, e * HEADS)
                    for k in range(HEADS):
                        last = nc.tensor.matmul(bank[7][:, :], gatw[:, k, :], nn[k], start=(k == 0), stop=(k == HEADS - 1))
                    last.then_inc(es_done, 1)
                if it == 3:
                    pe.wait_ge(sup_taken, e)
                    for b, gate in ((5, 0), (6, 1)):
                        last = nc.tensor.matmul(bank[b][:, :], wih[:, 0, gate, :], sup, start=False, stop=True)
                    last.then_inc(gate_done, 1)
                if it == 5:
                    pe.wait_ge(es_ready, e)
                    nc.tensor.matmul(bank[7][:, :], wih[:, 0, 2, :], sup, start=True, stop=True).then_inc(ni_done, 1)
                if it == 12:
                    pe.wait_ge(cand_ready, e * 2 - 1)
                    hidden(1)
                    for b, gate in ((5, 0), (6, 1)):
                        last = nc.tensor.matmul(bank[b][:, :], wih[:, 1, gate, :], es, start=False, stop=True)
                    last.then_inc(gate_done, 1)
                    nc.tensor.matmul(bank[7][:, :], wih[:, 1, 2, :], es, start=True, stop=True).then_inc(ni_done, 1)
                if it == 23:
                    pe.wait_ge(ysum_ready, e)
                    for q in range(QT):
                        last = nc.tensor.transpose(bank[4][:, q * P:(q + 1) * P], mix[:, q * P:(q + 1) * P], ident[:, :])
                    last.then_inc(yT_done, 1)

            pe.wait_ge(h_in, 16)
            pe.wait_ge(late_in, 96)
            for it in range(NT):
                tile(0, it)
            with pe.Fori(1, NC) as c:
                after(c, "start")
                for it in range(NT):
                    tile(c, it)
                    after(c, it)
            for it in ["start", *range(NT)]:
                after(NC, it)

        @block.scalar
        def _(act):
            act.wait_ge(v_done, 1)
            nc.scalar.copy(V[:, :], bank[7][:, 0:6]).then_inc(v_ready, 1)
            act.wait_ge(var_ready, 1)
            nc.scalar.activation(sq, sd, ACT.Sqrt).then_inc(sqrt_ready, 1)
            with act.Fori(0, NC // 2) as i:
                for b in range(2):
                    act.wait_ge(g0T_done, i * 2 + (b + 1))
                    nc.scalar.copy(gT[:, b, :], bank[b][:, :]).then_inc(g0T_ready, 1)
                for b in range(2):
                    act.wait_ge(S_done, i * 2 + (b + 1))
                    nc.scalar.copy(S[:, ds(i * 8 + b * 4, QT), :], bank[2 + b][:, :].rearrange("p (q d) -> p q d", q=QT))\
                      .then_inc(S_ready, 1)

            def signs(jc, groups):
                for g in groups:
                    act.wait_ge(a1_in[g % RING1], jc * (16 * NG1 // RING1) + 16 * (g // RING1 + 1))
                    act.wait_ge(code_ready, jc * NG1 + (g + 1))
                    nc.scalar.activation(sgn[:, g % 2, :], ring1[:, g % RING1, :, :], ACT.Sign).then_inc(a1_used_act, 1)

            def take_out(done):
                act.wait_ge(a1_used_pe, done * NG1)
                nc.scalar.activation(oT[:, :], bank[0][:, :], ACT.Relu, bias=b0[:, 0:1]).then_inc(oT_ready, 1)

            def root(done):
                act.wait_ge(var_ready, done)
                nc.scalar.activation(sq[:, 0:QT], sd[:, 0:QT], ACT.Sqrt).then_inc(sqrt_ready, 1)

            def take_hT(done):
                act.wait_ge(hT_done, done)
                act.wait_ge(hT_stored, done * 16)
                nc.scalar.copy(gT[:, 0, :], bank[2][:, :]).then_inc(hT_ready, 1)
                act.wait_ge(h_ready, done)
                act.dma_start(h_dram[ds(done - 1, 1), :, :].rearrange("o p j -> (o p) j"),
                              gx[:, 0:QT, :].rearrange("p q d -> p (q d)")).then_inc(h_stored, 16)
                act.wait_ge(hT_ready, done)
                act.dma_start(hT_dram[ds(done - 1, 1), :, :].rearrange("o p j -> (o p) j"), gT[:, 0, :]).then_inc(hT_stored, 16)

            signs(0, range(NG1))
            with act.Fori(1, NC) as jc:
                take_out(jc)
                signs(jc, range(0, 5))
                root(jc + 1)
                signs(jc, range(5, 10))
                take_hT(jc)
                signs(jc, range(10, NG1))
            take_out(NC)
            root(NC + 1)
            take_hT(NC)
            act.wait_ge(h_stored, 16 + 16 * NC)
            for n in range(3):
                act.wait_ge(arg_ready, n + 1)
                nc.scalar.activation(ww, tt, ACT.Exp).then_inc(exp_ready, 1)

            act.wait_ge(flags_ready, 1)
            wide = act.value_load(is_wide, min_val=0, max_val=1)
            with act.If(wide > 0):
                with act.Fori(0, NC) as c:
                    for it in range(NT):
                        for s in range(2):
                            for k in range(HEADS):
                                at = slice(k * CH, (k + 1) * CH)
                                act.wait_ge(wide_arg, c * (NT * 2 * HEADS) + ((it * 2 + s) * HEADS + k + 1))
                                nc.scalar.activation(wide_expo[:, at], wide_args[:, at], ACT.Exp,
                                                     bias=scores[:, it, s * HEADS + k:s * HEADS + k + 1]).then_inc(wide_exp, 1)
                    act.wait_ge(wide_rows, c + 1)
                    for k in range(HEADS):
                        at = slice(k * CH, (k + 1) * CH)
                        act.dma_start(guard_dram[k:k + 1, ds(c * CH, CH)], wide_ng[0:1, at]).then_inc(wide_stored, 16)
                        act.dma_start(rden_dram[k:k + 1, ds(c * CH, CH)], wide_args[0:1, at]).then_inc(wide_stored, 16)
                act.wait_ge(wide_stored, 32 * HEADS * NC)
                act.sem_inc(wide_done, 1)
            with act.Else():
                act.sem_inc(act_idle, 1)

            def exponentials(c, it):
                for k in range(HEADS):
                    n = c * (NT * HEADS) + (it * HEADS + k + 1)
                    act.wait_ge(arg4_ready, n)
                    act.wait_ge(w_ready, n)
                    nc.scalar.activation(expo[:, it % 2, k, :], args[:, it % 2, k, :], ACT.Exp,
                                         bias=scores[:, it, k:k + 1]).then_inc(e_ready, 1)

            def after(e, it):
                if it == 2:
                    act.wait_ge(tile_done, e * NT + 4)
                    nc.scalar.copy(sup, bank[3][:, :]).then_inc(sup_taken, 1)
                if it == 4:
                    act.wait_ge(es_done, e)
                    nc.scalar.copy(es, bank[7][:, :]).then_inc(es_ready, 1)
                for cell, at in ((0, 6), (1, 14)):
                    n = e * 2 - (1 - cell)
                    if it == at:
                        act.wait_ge(gate_done, n)
                        if cell == 1:
                            act.wait_ge(y_ready, n - 1)
                        nc.scalar.activation(gate_r, bank[5][:, :], ACT.Tanh, scale=0.5, bias=hbias[:, 2 * cell:2 * cell + 1])\
                          .then_inc(act_gate, 1)
                        nc.scalar.activation(gate_z, bank[6][:, :], ACT.Tanh, scale=0.5, bias=hbias[:, 2 * cell + 1:2 * cell + 2])\
                          .then_inc(act_gate, 1)
                    if it == at + 3:
                        act.wait_ge(pre_ready, n)
                        nc.scalar.activation(cell_n, cand, ACT.Tanh, bias=bias[:, 6 * cell + 2:6 * cell + 3])\
                          .then_inc(cand_ready, 1)
                if it == 28:
                    act.wait_ge(ot_ready, e)
                    act.dma_start(out_v[ds(e - 1, 1)].rearrange("o p q d -> (o p) q d"), ot.rearrange("p (q d) -> p q d", q=QT))\
                       .then_inc(out_stored, 16)

            def act_chunk(c, e=None):
                for it in range(NT):
                    exponentials(c, it)
                    if e is not None:
                        after(e, it)

            act.wait_ge(hb_ready, 1)
            act_chunk(0)
            with act.Fori(1, NC) as c:
                act_chunk(c, c)
            for it in range(NT):
                after(NC, it)
            act.wait_ge(out_stored, 16 + 16 * NC)

        @block.vector
        def _(dve):
            own = Chain(dve, dve_own, dve_idle)
            dve.sem_inc(code_ready, 2)
            for i in range(2):
                dve.wait_ge(xin_done[i], 16)
                for t in range(i * NT // 2, (i + 1) * NT // 2):
                    own.step(nc.vector.bn_stats(stats[:, t, :], x1[:, t, :]), wait=False)
            dve.wait_ge(dve_own, own.at)
            for t in range(NT):
                own.step(nc.vector.bn_aggr(mv[:, t, :], stats[:, t, :]), wait=(t == NT - 1))

            def variance(n):
                nc.vector.tensor_scalar(sd[:, 0:n], mv[:, 0:n, 1], EPS, None, ALU.add).then_inc(var_ready, 1)

            def inverse_root(n):
                own.step(nc.vector.reciprocal(rstd[:, 0:n], sq[:, 0:n]))
                own.step(nc.vector.tensor_tensor(rstd[:, 0:n], rstd[:, 0:n], sd[:, 0:n], ALU.mult))
                own.step(nc.vector.tensor_tensor(sq[:, 0:n], rstd[:, 0:n], sq[:, 0:n], ALU.add))
                own.step(nc.vector.tensor_scalar(sq[:, 0:n], sq[:, 0:n], 0.5, None, ALU.mult))
                own.step(nc.vector.reciprocal(rstd[:, 0:n], sq[:, 0:n]))

            def ln_relu(dst0, src, mean, scale):
                for q in range(QT):
                    own.step(nc.vector.tensor_scalar(gx[:, dst0 + q, :], src(q), mean(q), scale(q),
                                                     ALU.subtract, ALU.mult), wait=(q == QT - 1))

            variance(NT)
            dve.wait_ge(var_ready, 1)
            dve.wait_ge(sqrt_ready, 1)
            inverse_root(NT)
            for i in range(NC):
                b = i % 2
                if i >= 2:
                    dve.wait_ge(g0T_done, i - 1)
                ln_relu(b * QT, lambda q: x1[:, i * QT + q, :], lambda q: mv[:, i * QT + q, 0:1],
                        lambda q: rstd[:, i * QT + q:i * QT + q + 1])
                nc.vector.tensor_scalar(gx[:, b * QT:(b + 1) * QT, :], gx[:, b * QT:(b + 1) * QT, :], 0.0, None, ALU.max)\
                  .then_inc(g0_ready, 1)

            def codes(jc, groups):
                for g in groups:
                    dve.wait_ge(a1_used_act, jc * NG1 + (g + 1))
                    nc.vector.tensor_scalar(
                        big[:, :].rearrange("p (t j) -> p t j", t=NT)[:, g * GRP1:(g + 1) * GRP1, ds(jc * CH, CH)],
                        sgn[:, g % 2, :].rearrange("p (t j) -> p t j", t=GRP1), CODE_STEP, CODE_ZERO,
                        ALU.mult, ALU.add).then_inc(code_ready, 1)

            def residual(done):
                dve.wait_ge(o_nat, done)
                c = x1[:, ds(done * QT - QT, QT), :]
                own.step(nc.vector.tensor_tensor(c, c, bank[1][:, :].rearrange("p (q d) -> p q d", q=QT), ALU.add))
                own.stand()
                for q in range(QT):
                    own.step(nc.vector.bn_stats(stats[:, q, :], x1[:, ds(done * QT - QT + q, 1), :]), wait=(q == QT - 1))
                own.stand()
                for q in range(QT):
                    own.step(nc.vector.bn_aggr(mv[:, q, :], stats[:, q, :]), wait=(q == QT - 1))
                variance(QT)

            def normalise(done):
                dve.wait_ge(var_ready, done + 1)
                dve.wait_ge(sqrt_ready, done + 1)
                inverse_root(QT)
                dve.wait_ge(h_stored, done * 16)
                ln_relu(0, lambda q: x1[:, ds(done * QT - QT + q, 1), :], lambda q: mv[:, q, 0:1],
                        lambda q: rstd[:, q:q + 1])
                nc.vector.tensor_scalar(gx[:, 0:QT, :], gx[:, 0:QT, :], 0.0, None, ALU.max).then_inc(h_ready, 1)

            def take_u(done):
                dve.wait_ge(u_done, done)
                nc.vector.tensor_copy(u6[:, ds(done * QT - QT, QT), :],
                                      bank[3][:, 0:32].rearrange("p (q s) -> p q s", q=QT)[:, :, 0:6]).then_inc(u_ready, 1)

            codes(0, range(NG1))
            dve.wait_ge(g0T_done, NC)
            base = own.at
            with dve.Fori(1, NC) as jc:
                own.at = jc * OWN1 + (base - OWN1)
                codes(jc, range(0, 4))
                residual(jc)
                codes(jc, range(4, 6))
                normalise(jc)
                codes(jc, range(6, 13))
                take_u(jc)
                codes(jc, range(13, NG1))
            own.at = base + OWN1 * (NC - 1)
            residual(NC)
            normalise(NC)
            take_u(NC)
            assert own.at == base + OWN1 * NC, own.at - base

            dve.wait_ge(code_ready, 2 + NG1 * NC)
            diag = big[:, :].rearrange("p (b j) -> p b j", j=P)[:, ::NT + 1, :]
            own.step(nc.vector.tensor_tensor(diag, diag, notI[:, None, :].to_broadcast([P, NT, P]), ALU.mult), wait=False)

            def pieces(value, piece, rest):
                own.step(nc.vector.tensor_copy(piece(0), value))
                own.step(nc.vector.tensor_tensor(rest, value, piece(0), ALU.subtract))
                own.step(nc.vector.tensor_copy(piece(1), rest))
                own.step(nc.vector.tensor_tensor(piece(2), rest, piece(1), ALU.subtract))

            dve.wait_ge(u_ready, NC)
            flat = lambda a: a.rearrange("p t s -> p (t s)")
            own.step(nc.vector.tensor_scalar(mm[:, 0:NT * 6], flat(u6), 1 / POS_VALUE, None, ALU.mult))
            mvU5 = mvU[:, :, :, :].rearrange("p s t (c r) -> p s t c r", r=3)
            split = lambda a: a.rearrange("p (t c) -> p t c", t=NT)
            pieces(split(mm[:, 0:NT * 6]), lambda r: mvU5[:, 0, :, 0:6, r], split(tt[:, 0:NT * 6]))
            own.step(nc.vector.memset(mvU[:, 0, :, 18:21], 0.0), wait=False)
            own.step(nc.vector.memset(mvU[:, 1, :, 19:21], 0.0), wait=False)
            own.step(nc.vector.memset(mvU[:, 1, :, 18:19], 1 / NEG_VALUE), wait=False)
            own.step(nc.vector.tensor_scalar(mvU[:, 1, :, 0:9], mvU[:, 0, :, 9:18], POS_VALUE / NEG_VALUE, None, ALU.mult), wait=False)
            nc.vector.tensor_scalar(mvU[:, 1, :, 9:18], mvU[:, 0, :, 0:9], POS_VALUE / NEG_VALUE, None, ALU.mult)\
              .then_inc(mv_ready, 1)

            def make_masks(n, b, turn0):
                dve.wait_ge(mask_used, n + (turn0 + 1))
                nc.vector.tensor_scalar(masks32[:, b, 0, :, :], code32[:, :, ds(n * (P // 4), P // 4)], POS_BITS, None,
                                        ALU.bitwise_and)
                nc.vector.tensor_scalar(masks32[:, b, 1, :, :], code32[:, :, ds(n * (P // 4), P // 4)], NEG_BITS, None,
                                        ALU.bitwise_and).then_inc(mask_ready, 1)

            def take_sums(n, b, turn0, cols, dst):
                dve.wait_ge(mask_used, n + (turn0 + 3))
                nc.vector.tensor_reduce(dst[:, ds(n, 1), :], bank[b][:, 0:cols].rearrange("p (c r) -> p c r", r=3),
                                        AX.X, ALU.add).then_inc(sums_taken, 1)

            def mask_sums(turn0, cols, dst):
                make_masks(0, 0, turn0)
                with dve.Fori(0, NT // 2 - 1) as i:
                    make_masks(i * 2 + 1, 1, turn0)
                    take_sums(i * 2, 0, turn0, cols, dst)
                    make_masks(i * 2 + 2, 0, turn0)
                    take_sums(i * 2 + 1, 1, turn0, cols, dst)
                make_masks(NT - 1, 1, turn0)
                take_sums(NT - 2, 0, turn0, cols, dst)
                take_sums(NT - 1, 1, turn0, cols, dst)
                dve.wait_ge(sums_taken, turn0 + 2 + NT)

            dve.wait_ge(S_free, 1)
            dve.wait_ge(dve_own, own.at)
            mask_sums(0, 21, scores)
            own.step(nc.vector.scalar_tensor_tensor(flat(scores), flat(scores), ALPHA, flat(scores), ALU.mult, ALU.max))
            pos, neg = scores[:, :, 0:HEADS], scores[:, :, HEADS:2 * HEADS]
            own.step(nc.vector.tensor_tensor(delta, neg, pos, ALU.subtract), wait=False)

            both = scores[:, :, 0:2 * HEADS].rearrange("p t k -> p k t")
            own.step(nc.vector.tensor_reduce(tops[:, 0:6], both, AX.X, ALU.max), wait=False)
            own.step(nc.vector.tensor_reduce(tops[:, 6:12], both, AX.X, ALU.min, negate=True), wait=False)
            nc.vector.tensor_reduce(tops[:, 12:13], scores[:, :, 6:7].rearrange("p t k -> p k t"), AX.X, ALU.max)\
              .then_inc(ext_ready, 1)
            dve.wait_ge(all_ext, 1)
            own.step(nc.vector.tensor_scalar(tops[:, 29:30], tops[:, 28:29], 1.0, None, ALU.min))
            own.step(nc.vector.tensor_scalar(tops[:, 29:30], tops[:, 29:30], 1.0, HUGE, ALU.subtract, ALU.mult))
            for at in (16, 22):
                own.step(nc.vector.tensor_scalar(tops[:, at + 3:at + 6], tops[:, at + 3:at + 6], tops[:, 29:30], None, ALU.add), wait=False)
            dve.wait_ge(dve_own, own.at)
            for at in (16, 22):
                own.step(nc.vector.tensor_tensor(tops[:, at:at + 3], tops[:, at:at + 3], tops[:, at + 3:at + 6], ALU.max), wait=False)
            dve.wait_ge(dve_own, own.at)
            own.step(nc.vector.tensor_tensor(tops[:, 64:67], tops[:, 16:19], tops[:, 22:25], ALU.add), wait=False)
            own.step(nc.vector.tensor_tensor(tops[:, 67:70], tops[:, 16:19], tops[:, 22:25], ALU.max))
            own.step(nc.vector.tensor_scalar(tops[:, 64:67], tops[:, 64:67], WIN * WIDTH - 4.0, None, ALU.is_gt), wait=False)
            own.step(nc.vector.tensor_scalar(tops[:, 67:70], tops[:, 67:70], COARSE, None, ALU.is_gt))
            own.step(nc.vector.tensor_reduce(tops[:, 70:71], tops[:, 64:70], AX.X, ALU.max), wait=False)
            own.step(nc.vector.tensor_scalar(tops[:, 71:72], tops[:, 28:29], 1.0, None, ALU.min))
            nc.vector.tensor_copy(tops[:, 72:74].bitcast(I32), tops[:, 70:72]).then_inc(flags_ready, 1)
            own.step(nc.vector.tensor_copy(tops[:, 32:35].bitcast(I32), tops[:, 16:19]))
            own.step(nc.vector.tensor_copy(tops[:, 36:39], tops[:, 32:35].bitcast(I32)))
            bg = tops[:, 40:40 + KG].rearrange("p (k g) -> p k g", k=HEADS)
            for g in range(WIN):
                own.step(nc.vector.tensor_scalar(bg[:, :, g], tops[:, 36:39], 1.0 - WIDTH / 2 - WIDTH * g, None, ALU.add),
                         wait=(g == WIN - 1))
            t4 = tt.rearrange("p (t k g) -> p t k g", t=NT, k=HEADS)
            for s, (e, value) in enumerate(((pos, POS_VALUE), (neg, NEG_VALUE))):
                bgb = bg[:, None, :, :].to_broadcast([P, NT, HEADS, WIN])
                own.step(nc.vector.tensor_tensor(t4, e[:, :, :, None].to_broadcast([P, NT, HEADS, WIN]), bgb, ALU.subtract))
                own.step(nc.vector.tensor_scalar(mm, tt, -WIDTH / 2, 1 / value, ALU.is_gt, ALU.mult))
                own.step(nc.vector.scalar_tensor_tensor(mm, tt, WIDTH / 2, mm, ALU.is_le, ALU.mult), wait=False)
                nc.vector.tensor_scalar(tt, tt, WIDTH / 2, -WIDTH / 2, ALU.min, ALU.max).then_inc(arg_ready, 1)
                dve.wait_ge(exp_ready, s + 1)
                dve.wait_ge(dve_own, own.at)
                own.step(nc.vector.tensor_tensor(ww, ww, mm, ALU.mult))
                pieces(ww, lambda r: mvW[:, s, :, :].rearrange("p t (c r) -> p (t c) r", r=3)[:, :, r], ww)
            nc.vector.memset(tops[:, 39:40], 0.0).then_inc(mv_ready, 1)
            mask_sums(NT, KG * 3, wsum)

            ws = flat(wsum)
            own.step(nc.vector.tensor_scalar(tt.bitcast(I32), ws.bitcast(I32), 23, None, ALU.logical_shift_right))
            own.step(nc.vector.tensor_copy(mm, tt.bitcast(I32)))
            own.step(nc.vector.tensor_scalar(tt, mm, 0.0, -HUGE, ALU.is_equal, ALU.mult), wait=False)
            own.step(nc.vector.tensor_scalar(mm, mm, LN2, -126 * LN2, ALU.mult, ALU.add))
            own.step(nc.vector.tensor_tensor(tt, tt, mm, ALU.add))
            own.step(nc.vector.tensor_tensor(t4, t4, bgb, ALU.add))
            gd = guard
            rd = rden
            own.step(nc.vector.tensor_reduce(gd, tt.rearrange("p (c g) -> p c g", g=WIN), AX.X, ALU.max))
            gdb = gd.rearrange("p (t k) -> p t k", t=NT)[:, :, :, None].to_broadcast([P, NT, HEADS, WIN])
            own.step(nc.vector.tensor_tensor(t4, bgb, gdb, ALU.subtract), wait=False)
            ngd = nguard
            own.step(nc.vector.tensor_scalar(ngd, gd, -1.0, None, ALU.mult))
            nc.vector.tensor_scalar(tt, tt, 80.0, None, ALU.min).then_inc(arg_ready, 1)
            dve.wait_ge(exp_ready, 3)
            own.step(nc.vector.tensor_tensor(ww, ww, ws, ALU.mult))
            own.step(nc.vector.tensor_reduce(rd, ww.rearrange("p (c g) -> p c g", g=WIN), AX.X, ALU.add))
            own.step(nc.vector.tensor_scalar(rd, rd, 1e-20, float(HEADS), ALU.max, ALU.mult))
            nc.vector.reciprocal(rd, rd).then_inc(nat_ready, 1)
            dve.wait_ge(rows_done, 1)
            nc.vector.tensor_copy(rows[:, :, :], bank[2][0:HEADS * NT, 0:2 * P].rearrange("p (s j) -> p s j", s=2))\
              .then_inc(rows_ready, 1)

            dve.wait_ge(flags_ready, 1)
            wide = dve.value_load(is_wide, min_val=0, max_val=1)
            with dve.If(wide > 0):
                wo = Chain(dve, wide_own, dve_idle)
                bound = (caps, rden.rearrange("p (t k) -> p t k", t=NT))
                for b, e in zip(bound, (pos, neg)):
                    wo.step(nc.vector.tensor_scalar(b, e, -1.0, CAP, ALU.mult, ALU.add), wait=False)
                wo.step(nc.vector.memset(all_ones, 1.0))
                at0 = wo.at
                head = lambda a, k: a[:, k * CH:(k + 1) * CH]
                with dve.Fori(0, NC) as c:
                    wo.at = c * WIDE_OWN + at0
                    code = lambda it: big[:, ds(c * CH + it * N, CH)]
                    wo.step(nc.vector.memset(wide_acc, -HUGE))
                    for it in range(NT):
                        wo.step(nc.vector.tensor_scalar(not_pos, code(it), POS_CODE, -HUGE, ALU.not_equal, ALU.mult), wait=False)
                        wo.step(nc.vector.tensor_scalar(not_neg, code(it), NEG_CODE, -HUGE, ALU.not_equal, ALU.mult))
                        for s, no_edge in enumerate((not_pos, not_neg)):
                            for k in range(HEADS):
                                wo.step(nc.vector.scalar_tensor_tensor(
                                    head(wide_acc, k), no_edge, scores[:, it, s * HEADS + k:s * HEADS + k + 1],
                                    head(wide_acc, k), ALU.add, ALU.max), wait=(k == HEADS - 1))
                    dve.sem_inc(wide_max, 1)
                    dve.wait_ge(wide_reduced, c + 1)
                    wo.step(nc.vector.tensor_scalar(wide_ng, wide_ng, -1.0, None, ALU.mult), wait=False)
                    wo.step(nc.vector.memset(wide_acc, 0.0))
                    for it in range(NT):
                        for s in range(2):
                            for k in range(HEADS):
                                nc.vector.tensor_scalar(head(wide_args, k), head(wide_ng, k), bound[s][:, it, k:k + 1], None, ALU.min)\
                                  .then_inc(wide_arg, 1)
                            for k in range(HEADS):
                                dve.wait_ge(wide_exp, c * (NT * 2 * HEADS) + ((it * 2 + s) * HEADS + k + 1))
                                dve.sem_inc(dve_idle, 1)
                                wo.step(nc.vector.scalar_tensor_tensor(head(wide_expo, k), code(it), (POS_CODE, NEG_CODE)[s],
                                                                       head(wide_expo, k), ALU.is_equal, ALU.mult))
                                wo.step(nc.vector.tensor_tensor(head(wide_acc, k), head(wide_acc, k), head(wide_expo, k), ALU.add))
                    dve.sem_inc(wide_sum, 1)
                    dve.wait_ge(wide_total, c + 1)
                    for k in range(HEADS):
                        wo.step(nc.vector.tensor_scalar(head(wide_args, k), bank[k][:, :], 1e-20, float(HEADS), ALU.max, ALU.mult),
                                wait=(k == HEADS - 1))
                    nc.vector.reciprocal(wide_args, wide_args).then_inc(wide_rows, 1)
                    dve.wait_ge(wide_stored, c * (32 * HEADS) + 32 * HEADS)
            with dve.Else():
                dve.sem_inc(dve_idle, 1)

            dve.wait_ge(late_in, 96)
            own.step(nc.vector.tensor_scalar(caps, pos, -1.0, CAP, ALU.mult, ALU.add), wait=False)
            b4 = bias.rearrange("p (c s g) -> p c s g", c=2, s=2)
            own.step(nc.vector.tensor_tensor(hbias.rearrange("p (c g) -> p c g", c=2), b4[:, :, 0, 0:2], b4[:, :, 1, 0:2], ALU.add))
            nc.vector.tensor_scalar(hbias, hbias, 0.5, None, ALU.mult).then_inc(hb_ready, 1)

            def find_neg(c, g):
                dve.wait_ge(a4_clean, c * NG + (g + 1))
                so.step(nc.vector.tensor_scalar(isneg, a4[:, g % RING, :, :].rearrange("p r j -> p (r j)"), 0.0, None, ALU.is_lt))

            def arguments(c, it, signed):
                for k in range(HEADS):
                    dve.wait_ge(e_ready, c * (NT * HEADS) + (it * HEADS + k + 1))
                    arg, row = args[:, it % 2, k, :], guard_row(c, k)
                    if signed:
                        so.step(nc.vector.scalar_tensor_tensor(arg, isneg[:, (it % GRP) * CH:(it % GRP + 1) * CH],
                                                                delta[:, it, k:k + 1], row, ALU.mult, ALU.add))
                        row = arg
                    nc.vector.tensor_scalar(arg, row, caps[:, it, k:k + 1], None, ALU.min).then_inc(arg4_ready, 1)

            def guard_row(c, k):
                return ngB[:, k, :] if isinstance(c, int) and c == 0 else \
                    ngB[:, ds((c % 2) * HEADS + k, 1), :].rearrange("p o j -> p (o j)")

            def weights(c, it):
                for k in range(HEADS):
                    dve.wait_ge(e_ready, c * (NT * HEADS) + (6 + it * HEADS + k + 1))
                    if k == 0:
                        dve.wait_ge(tile_done, c * NT + (it + 1))
                        if it % GRP == 0:
                            dve.wait_ge(a4_clean, c * NG + (it // GRP + 1))
                    nc.vector.tensor_tensor(wgt[:, it % RING, k, :], expo[:, it % 2, k, :],
                                            a4[:, (it // GRP) % RING, it % GRP, :], ALU.mult)\
                      .then_inc(w_ready, 1)

            def after(e, it):
                if it == 2:
                    dve.wait_ge(tile_done, e * NT + 4)
                    for k in range(HEADS):
                        nc.vector.tensor_tensor(nn[k], bank[k][:, :],
                                                rdB[:, ds(((e - 1) % 2) * HEADS + k, 1), :].rearrange("p o j -> p (o j)"),
                                                ALU.mult).then_inc(nn_taken, 1)
                for cell, at in ((0, 6), (1, 14)):
                    n = e * 2 - (1 - cell)
                    if it == at:
                        dve.wait_ge(ni_done, n)
                        own.step(nc.vector.tensor_scalar(cand, bank[4][:, :], bias[:, 6 * cell + 5:6 * cell + 6], 0.5,
                                                         ALU.add, ALU.mult))
                    if it == at + 1:
                        dve.wait_ge(act_gate, n * 2 - 1)
                        own.step(nc.vector.scalar_tensor_tensor(cand, gate_r, 1.0, cand, ALU.add, ALU.mult))
                        nc.vector.tensor_tensor(cand, cand, bank[7][:, :], ALU.add).then_inc(pre_ready, 1)
                    if it == at + 5:
                        dve.wait_ge(diff_ready, n)
                        dve.wait_ge(act_gate, n * 2)
                        own.step(nc.vector.scalar_tensor_tensor(mix, gate_z, 1.0, mix, ALU.add, ALU.mult))
                        nc.vector.scalar_tensor_tensor(mix if cell else y_edge, mix, 0.5, cell_n, ALU.mult, ALU.add)\
                          .then_inc(y_ready, 1)
                if it == 26:
                    dve.wait_ge(yT_done, e)
                    dve.wait_ge(out_stored, e * 16)
                    own.stand()
                    for q in range(QT):
                        j = e * QT - (QT - q)
                        ins_ = nc.vector.scalar_tensor_tensor(ot[:, q * P:(q + 1) * P], bank[4][:, q * P:(q + 1) * P],
                                                              dg[:, ds(j, 1)], x1[:, ds(j, 1), :].rearrange("p o d -> p (o d)"),
                                                              ALU.mult, ALU.add)
                    ins_.then_inc(ot_ready, 1)

            def dve_chunk(c, signed, e=None):
                if signed:
                    find_neg(c, 0)
                arguments(c, 0, signed)
                for it in range(NT):
                    if it + 1 < NT:
                        if signed and (it + 1) % GRP == 0:
                            find_neg(c, (it + 1) // GRP)
                        arguments(c, it + 1, signed)
                    weights(c, it)
                    if e is not None:
                        after(e, it)

            def all_chunks(signed):
                dve.wait_ge(gd_in[0], 32)
                dve_chunk(0, signed)
                base = own.at
                with dve.Fori(1, NC) as c:
                    own.at = c * OWN4 + (base - OWN4)
                    so.at = c * SIGNED_OWN
                    dve.wait_ge(gd_in[0], c * 32 + 32)
                    dve_chunk(c, signed, c)
                own.at = base + OWN4 * (NC - 1)
                for it in range(NT):
                    after(NC, it)
                assert own.at == base + OWN4 * NC

            so = Chain(dve, signed_own, dve_idle)
            negatives = dve.value_load(is_signed, min_val=0, max_val=1)
            start = own.at
            with dve.If(negatives > 0):
                all_chunks(True)
            own.at = start
            with dve.Else():
                all_chunks(False)

        @block.gpsimd
        def _(pool):
            nc.gpsimd.memset(ident[:, :], 0.0).then_inc(pool_own, 1)
            pool.wait_ge(pool_own, 1)
            nc.gpsimd.affine_select(out=ident[:, :], in_=ident[:, :], compare_op=ALU.not_equal, fill=1.0, base=0,
                                    pattern=[[-1, P]], channel_multiplier=1).then_inc(const_ready, 1)
            pool.wait_ge(const_ready, 1)
            nc.gpsimd.tensor_scalar(notI[:, :], ident[:, :], -1.0, 1.0, ALU.mult, ALU.add).then_inc(const_ready, 1)
            pool.sem_inc(h_stored, 16)
            pool.sem_inc(hT_stored, 16)
            pool.sem_inc(mask_used, 2)
            pool.sem_inc(sums_taken, 2)
            pool.sem_inc(tile_done, RING)
            pool.sem_inc(e_ready, 2 * HEADS)
            pool.sem_inc(w_ready, 2 * HEADS)
            pool.sem_inc(out_stored, 16)
            pool.wait_ge(ext_ready, 1)
            nc.gpsimd.partition_all_reduce(tops[:, 16:29], tops[:, 0:13], P, RMAX).then_inc(all_ext, 1)
            pool.wait_ge(u_ready, NC)
            nc.gpsimd.memset(offdiag, 1.0).then_inc(offd_ready, 1)
            pool.wait_ge(offd_ready, 1)
            nc.gpsimd.tensor_copy(offdiag[:, (NC - 1) * P:NC * P], notI[:, :]).then_inc(offd_ready, 1)
            pool.wait_ge(offd_ready, 2)
            pool.wait_ge(xdg_in, 16)

            pool.wait_ge(flags_ready, 1)
            wide = pool.value_load(is_wide, min_val=0, max_val=1)
            with pool.If(wide > 0):
                with pool.Fori(0, NC) as c:
                    pool.wait_ge(wide_max, c + 1)
                    pool.sem_inc(pool_idle, 1)
                    nc.gpsimd.partition_all_reduce(wide_ng, wide_acc, P, RMAX).then_inc(wide_reduced, 1)
            with pool.Else():
                pool.sem_inc(pool_idle, 1)

            def clean(c, g):
                pool.wait_ge(a4_in[g % RING], c * (16 * NG // RING) + 16 * (g // RING + 1))
                pool.sem_inc(pool_idle, 1)
                blocks = a4[:, g % RING, :, :].rearrange("p r (b j) -> p (r b) j", j=P)[:, ::QT + 1, :]
                at = (NC - 1 + g - c) * P
                m = offdiag[:, at:at + P] if isinstance(c, int) else offdiag[:, ds(at, P)]
                nc.gpsimd.tensor_tensor(blocks, blocks, m[:, None, :].to_broadcast([P, GRP, P]), ALU.mult).then_inc(a4_clean, 1)

            def after(e, it):
                for cell, at in ((0, 10), (1, 18)):
                    n = e * 2 - (1 - cell)
                    if it == at:
                        pool.wait_ge(cand_ready, n)
                        if cell == 1:
                            pool.wait_ge(y_ready, n - 1)
                        pool.sem_inc(pool_idle, 1)
                        nc.gpsimd.tensor_tensor(mix, hTc, cell_n, ALU.subtract).then_inc(diff_ready, 1)
                if it == 20:
                    pool.wait_ge(y_ready, e * 2)
                    pool.sem_inc(pool_idle, 1)
                    nc.gpsimd.tensor_tensor(mix, mix, y_edge, ALU.add).then_inc(ysum_ready, 1)

            def pool_chunk(c, e=None):
                clean(c, 0)
                clean(c, 1)
                for it in range(NT):
                    if it % GRP == 1 and it // GRP + 2 < NG:
                        clean(c, it // GRP + 2)
                    if e is not None:
                        after(e, it)

            pool_chunk(0)
            with pool.Fori(1, NC) as c:
                pool_chunk(c, c)
            for it in range(NT):
                after(NC, it)




def kernel(**inputs):
    import numpy as np
    import concourse.bacc as bacc
    from concourse.bass_utils import run_bass_kernel_spmd

    a = {k: np.asarray(v) for k, v in inputs.items()}
    sent = {
        "x": a["x"],
        "adjT": a["adj"].T.reshape(NT, P, NC, CH).transpose(2, 1, 0, 3),
        "L0_gnn_W": a["L0_gnn_W"],
        "L0_gnn_b": a["L0_gnn_b"],
        "gat_W": a["L1_gnn_gat_W"].transpose(1, 0, 2),
        "gat_WT": a["L1_gnn_gat_W"].transpose(0, 2, 1),
        "gat_a": a["L1_gnn_gat_a"].reshape(HEADS, 2, P).transpose(2, 1, 0).reshape(P, 2 * HEADS),
        "diag": a["adj"].diagonal().reshape(NT, P).T,
        "bias": np.stack([a[f"L1_gnn_{c}_{b}"].reshape(3, P) for c in ("edge", "node") for b in ("bih", "bhh")])
                  .reshape(12, P).T,
        **{f"{c}_{w}T": a[f"L1_gnn_{c}_{w}"].reshape(3, P, P).transpose(2, 0, 1) for c in ("edge", "node") for w in ("Wih", "Whh")},
    }
    nc = bacc.Bacc("TRN2", target_bir_lowering=False, num_devices=1)
    arrays, ins = {}, {}
    for name, value in sent.items():
        arrays[f"in_{name}"] = np.ascontiguousarray(value)
        ins[name] = nc.dram_tensor(f"in_{name}", value.shape, mybir.dt.from_np(value.dtype), kind="ExternalInput").ap()
    out = nc.dram_tensor("out", (N, P), F32, kind="ExternalOutput").ap()
    build(nc, ins, out)
    r = run_bass_kernel_spmd(nc, [arrays], core_ids=[0])
    return r.results[0]["out"]
```

```python
from contextlib import ExitStack

import concourse.bass as bass
from concourse import mybir
from concourse.bass import ds

F32 = mybir.dt.float32
BF16 = mybir.dt.bfloat16
FP8 = mybir.dt.float8e4
U8 = mybir.dt.uint8
U32 = mybir.dt.uint32
I32 = mybir.dt.int32
ALU = mybir.AluOpType
ACT = mybir.ActivationFunctionType
AX = mybir.AxisListType

P = 128
N = 4096
NT = N // P
CH = 512
NC = N // CH
QT = CH // P
HEADS = 3
EPS = 1e-5
ALPHA = 0.2

GRP1 = 2
NG1 = NT // GRP1
RING1 = 4
ROUNDS = 4
RT = NT // ROUNDS
RG = RT // GRP1
GRP = 4
NG = NT // GRP
DEN_AT = 10
AHEAD = 9
RING = 4

CODE_STEP, CODE_ZERO = 80.0, 128.0
POS_CODE, NEG_CODE = CODE_ZERO + CODE_STEP, CODE_ZERO - CODE_STEP
POS_BITS, POS_VALUE = 0x40404040, 2.0
NEG_BITS, NEG_VALUE = 0x20202020, 0.125

WIN = 6
WIDTH = 140
KG = HEADS * WIN
RMAX = bass.bass_isa.ReduceOp.max
LN2 = 0.6931471805599453
MASKS = 4
HUGE = 1e30
COARSE = 1e6

WIDE_OWN = 2 + NT * (2 + 2 * HEADS) + 1 + NT * 2 * HEADS * 2 + HEADS
SIGNED_OWN = 2 * NG + 3 * NT * HEADS
OWN4 = 6
OWN1 = 1 + 2 * QT + 5 + QT + NG1


class Chain:

    def __init__(self, eng, sem, idle):
        self.eng, self.sem, self.idle, self.at = eng, sem, idle, 0

    def stand(self):
        self.eng.sem_inc(self.idle, 1)

    def step(self, ins, wait=True):
        ins.then_inc(self.sem, 1)
        self.at = self.at + 1
        if wait:
            self.eng.wait_ge(self.sem, self.at)


def build(nc, ins, out):
    ctx = ExitStack()
    with ctx:
        def sb(name, shape, dt):
            return ctx.enter_context(nc.sbuf_tensor(name, shape, dt))

        def sem(name):
            return ctx.enter_context(nc.semaphore(name))

        h_dram = nc.dram_tensor("h_scratch", (NC, P, QT * P), F32)
        hT_dram = nc.dram_tensor("hT_scratch", (NC, P, CH), F32)
        guard_dram = nc.dram_tensor("guard_scratch", (HEADS, N), F32)
        rden_dram = nc.dram_tensor("rden_scratch", (HEADS, N), F32)

        big = sb("big", [P, NT * N], U8)
        codes8 = big[:, :].rearrange("p (n t j) -> p n t j", n=NT, t=NT)
        code32 = big[:, :].bitcast(U32).rearrange("p (n t j) -> p n t j", n=NT, t=NT)
        x1 = sb("x1", [P, NT, P], F32)
        S = sb("S", [P, NT, P], F32)
        ring1 = sb("ring1", [P, RING1, GRP1, CH], F32)
        small = sb("small", [P, 1280], F32)
        vecs = sb("vecs", [P, NT * 25], F32)
        ident = sb("ident", [P, P], F32)
        notI = sb("notI", [P, P], U8)
        w0 = sb("w0", [P, P], F32)
        b0 = sb("b0", [P, 1], F32)
        wT = sb("wT", [P, HEADS, P], F32)
        av = sb("av", [P, 2 * HEADS], F32)
        V = sb("V", [P, 2 * HEADS], F32)
        gx = sb("gx", [P, QT * 2, P], F32)
        gT = sb("gT", [P, 2, CH], F32)
        oT = sb("oT", [P, CH], F32)
        sgn = sb("sgn", [P, 2, GRP1 * CH], BF16)

        wsum = sb("wsum", [P, NT, KG], F32)
        tops = sb("tops", [P, 96], F32)
        rows = sb("rows", [HEADS * NT, 2, P], F32)
        masks = S[:, :, :].bitcast(FP8).rearrange("p t j -> p (t j)").rearrange("p (b t j) -> p b t j", b=MASKS, t=NT)
        masks32 = S[:, :, :].bitcast(U32).rearrange("p t j -> p (t j)").rearrange("p (b t j) -> p b t j", b=MASKS, t=NT)
        r1 = ring1[:, :, :, :].rearrange("p a b c -> p (a b c)")
        mvW = r1[:, 0:2 * NT * KG * 3 // 2].bitcast(BF16).rearrange("p (s t c) -> p s t c", s=2, t=NT)
        tt = r1[:, 2304:2304 + NT * KG]
        mm = r1[:, 3072:3072 + NT * KG]
        t2 = wsum[:, :, :].rearrange("p t c -> p (t c)")
        ww = gx[:, :, :].rearrange("p a b -> p (a b)")[:, 0:NT * KG]
        mvU = sb("mvU", [P, 2, NT, 21], BF16)

        place = [0]

        def over(shape, dt=F32, size=4):
            n = 1
            for d in shape:
                n *= d
            a = big[:, place[0]:place[0] + n * size].bitcast(dt)
            place[0] += n * size
            names = " ".join(f"d{i}" for i in range(len(shape)))
            return a if len(shape) == 1 else a.rearrange(f"p ({names}) -> p {names}", **{f"d{i}": d for i, d in enumerate(shape)})

        a4 = over((RING, GRP, CH))
        h = over((NT, P))
        args = over((2, HEADS, CH))
        expo = over((2, HEADS, CH))
        wgt = over((RING, HEADS, CH))
        not_neg4 = over((GRP * CH,), BF16, 2)
        is_neg4 = over((GRP * CH,), BF16, 2)
        ngB = over((2 * HEADS, CH))
        rdB = over((2 * HEADS, CH))
        assert place[0] <= NT * N
        slots = [S[:, 4 * i:4 * i + 4, :].rearrange("p t j -> p (t j)") for i in range(8)] + \
                [ring1[:, i // 2, i % 2, :] for i in range(8)]
        nn, sup, es, hTc = slots[0:3], slots[3], slots[4], slots[5]
        gate_r, gate_z, cand, mix, y_edge, ot = slots[6], slots[7], slots[8], slots[9], slots[10], slots[11]
        cell_n = slots[12]

        def cell_banks(cell, last):
            return (0, 1, 2, 3) if last and cell == 1 else (4, 5, 6, 7)

        def cell_buffers(cell, last):
            return (args[:, 0, 0, :], args[:, 0, 1, :], expo[:, 0, 0, :], expo[:, 0, 1, :], expo[:, 0, 2, :]) \
                if last and cell == 1 else (cand, mix, gate_r, gate_z, cell_n)
        wih = gT[:, :, :].rearrange("p a b -> p (a b)")[:, 0:2 * 3 * P].rearrange("p (c g d) -> p c g d", c=2, g=3)
        whh = sgn[:, :, :].rearrange("p a b -> p (a b)").bitcast(F32)[:, 0:2 * 3 * P]\
            .rearrange("p (c g d) -> p c g d", c=2, g=3)
        gatw = oT[:, 0:HEADS * P].rearrange("p (k d) -> p k d", k=HEADS)
        offdiag = small[:, 0:(2 * NC - 1) * P // 2].bitcast(BF16)
        bias = small[:, 1000:1012]
        hbias = small[:, 1012:1016]
        dg = small[:, 1016:1016 + NT]

        s_flat = S[:, :, :].rearrange("p t j -> p (t j)")
        wide_acc = s_flat[:, 0:HEADS * CH]
        wide_ng = s_flat[:, HEADS * CH:2 * HEADS * CH]
        not_pos, not_neg = s_flat[:, 3072:3072 + CH], s_flat[:, 3072 + CH:3072 + 2 * CH]
        wide_args, wide_expo = r1[:, 0:HEADS * CH], r1[:, HEADS * CH:2 * HEADS * CH]
        all_ones = r1[:, 3840:3840 + P]
        gdiag = [s_flat[:, k * CH:(k + 1) * CH] for k in range(HEADS)]
        cap = tops[:, 74:75]
        below = tops[:, 86:86 + WIN]
        any_neg = tops[0:1, 82:83].bitcast(I32)
        bits_flat = wsum[:, :, :].rearrange("p t c -> p (t c)")[:, 0:GRP1 * CH // 4]
        any_bits = bits_flat.bitcast(U32).rearrange("p (n t j) -> p n t j", n=QT, t=GRP1)
        is_wide, is_signed = tops[0:1, 72:73].bitcast(I32), tops[0:1, 73:74].bitcast(I32)

        stats = small[:, 0:NT * 6].rearrange("p (t s) -> p t s", t=NT)
        mv = small[:, 192:192 + NT * 2].rearrange("p (t s) -> p t s", t=NT)
        sd = small[:, 256:288]
        sq = small[:, 288:320]
        rstd = small[:, 320:352]
        u6 = vecs[:, 0:NT * 6].rearrange("p (t s) -> p t s", t=NT)
        scores = vecs[:, NT * 6:NT * 13].rearrange("p (t s) -> p t s", t=NT)
        kept = vecs[:, NT * 13:NT * 16].rearrange("p (t s) -> p t s", t=NT)
        guard = vecs[:, NT * 16:NT * 19]
        rden = vecs[:, NT * 19:NT * 22]
        caps = guard.rearrange("p (t k) -> p t k", t=NT)
        nguard = vecs[:, NT * 22:NT * 25]

        OUT = (0, 6)
        bank = [ctx.enter_context(nc.psum_tensor(f"bank{i}", [P, CH], F32)) for i in range(8)]

        xin_done = [None] + [sem(f"xin_done{i}") for i in range(1, ROUNDS)]
        w0_in = sem("w0_in")
        x0_in = [sem(f"x0_in{b}") for b in range(2)]
        consts_in = sem("consts_in")
        const_ready = sem("const_ready")
        v_done = sem("v_done")
        v_ready = sem("v_ready")
        dve_own = sem("dve_own")
        dve_idle, pe_idle, pool_idle = sem("dve_idle"), sem("pe_idle"), sem("pool_idle")
        var_ready = sem("var_ready")
        sqrt_ready = sem("sqrt_ready")
        g0_ready = sem("g0_ready")
        g0T_done = sem("g0T_done")
        g0T_ready = sem("g0T_ready")
        S_done = sem("S_done")
        S_ready = sem("S_ready")
        a1_in = [sem(f"a1_in{i}") for i in range(RING1)]
        a1_used_pe = sem("a1_used_pe")
        a1_used_act = sem("a1_used_act")
        code_ready = sem("code_ready")
        oT_ready = sem("oT_ready")
        o_nat = sem("o_nat")
        h_ready = sem("h_ready")
        h_stored = sem("h_stored")
        hT_done = sem("hT_done")
        hT_ready = sem("hT_ready")
        hT_stored = sem("hT_stored")
        u_done = sem("u_done")
        u_ready = sem("u_ready")
        u_pos_ready, u_neg_ready = sem("u_pos_ready"), sem("u_neg_ready")
        w_pos_ready, w_neg_ready = sem("w_pos_ready"), sem("w_neg_ready")
        mask_ready = sem("mask_ready")
        mask_used = sem("mask_used")
        sums_taken = sem("sums_taken")
        late_in = sem("late_in")
        a4_clean = sem("a4_clean")
        tile_done = sem("tile_done")
        arg4_ready = sem("arg4_ready")
        e_ready = sem("e_ready")
        w_ready = sem("w_ready")
        guard_stored = sem("guard_stored")
        h_in = sem("h_in")
        hT_in = sem("hT_in")
        sup_taken = sem("sup_taken")
        nn_taken = sem("nn_taken")
        es_done = sem("es_done")
        es_ready = sem("es_ready")
        gate_done = sem("gate_done")
        ni_done = sem("ni_done")
        act_gate = sem("act_gate")
        pre_ready = sem("pre_ready")
        cand_ready = sem("cand_ready")
        diff_ready = sem("diff_ready")
        y_ready = sem("y_ready")
        ysum_ready = sem("ysum_ready")
        yT_done = sem("yT_done")
        ot_ready = sem("ot_ready")
        out_stored = sem("out_stored")
        hb_ready = sem("hb_ready")
        offd_ready = sem("offd_ready")
        a4_in = [sem(f"a4_in{i}") for i in range(RING)]
        rows_in = sem("rows_in")
        ext_ready = sem("ext_ready")
        all_ext = sem("all_ext")
        arg_ready = sem("arg_ready")
        exp_ready = sem("exp_ready")
        nat_ready = sem("nat_ready")
        rows_done = sem("rows_done")
        rows_ready = sem("rows_ready")
        pool_own = sem("pool_own")
        xdg_in = sem("xdg_in")
        sp_idle, act_idle = sem("sp_idle"), sem("act_idle")
        flags_ready = sem("flags_ready")
        den_own = sem("den_own")
        gdiag_ready, g_spread, ng0_ready, ng0_in = sem("gdiag_ready"), sem("g_spread"), sem("ng0_ready"), sem("ng0_in")
        arg_neg_ready, exp_neg_ready = sem("arg_neg_ready"), sem("exp_neg_ready")
        neg_own = sem("neg_own")
        neg_found, neg_reduced, neg_known = sem("neg_found"), sem("neg_reduced"), sem("neg_known")
        wide_own = sem("wide_own")
        wide_max = sem("wide_max")
        wide_reduced = sem("wide_reduced")
        wide_arg = sem("wide_arg")
        wide_exp = sem("wide_exp")
        wide_sum = sem("wide_sum")
        wide_total = sem("wide_total")
        wide_rows = sem("wide_rows")
        wide_stored = sem("wide_stored")
        wide_done = sem("wide_done")
        signed_own = sem("signed_own")

        x_v = ins["x"].rearrange("(t p) d -> p t d", p=P)
        out_v = out.rearrange("(c q p) d -> c p q d", p=P, q=QT)
        aT_v = ins["adjT"]

        block = ctx.enter_context(nc.Block())

        @block.sync
        def _(sp):
            def load_x(i):
                part = slice(i * RT, (i + 1) * RT)
                sp.dma_start(x1[:, part, :], x_v[:, part, :]).then_inc(xin_done[i], 16)

            def load1(jc, g):
                sp.dma_start(ring1[:, g % RING1, :, :], aT_v[jc, :, g * GRP1:(g + 1) * GRP1, :])\
                  .then_inc(a1_in[g % RING1], 16)

            for b in range(2):
                sp.dma_start(x1[:, b * QT:(b + 1) * QT, :], x_v[:, b * QT:(b + 1) * QT, :]).then_inc(x0_in[b], 16)
            sp.dma_start(w0[:, :], ins["L0_gnn_W"]).then_inc(w0_in, 16)
            load_x(1)
            load1(0, 0)
            load_x(2)
            load1(0, 1)
            load_x(3)
            load1(0, 2)
            sp.dma_start(b0[:, :], ins["L0_gnn_b"].rearrange("(p o) -> p o", o=1)).then_inc(consts_in, 16)
            sp.dma_start(wT[:, :, :], ins["gat_WT"].rearrange("k e d -> e k d")).then_inc(consts_in, 16)
            sp.dma_start(av[:, :], ins["gat_a"]).then_inc(consts_in, 16)
            load1(0, 3)
            sp.dma_start(dg, ins["diag"]).then_inc(xdg_in, 16)

            def steady(jc, groups):
                for g in range(groups):
                    sp.wait_ge(a1_used_pe, jc * NG1 + (g + 1))
                    sp.wait_ge(a1_used_act, jc * NG1 + (g + 1))
                    ahead = g + RING1
                    if ahead < NG1:
                        sp.dma_start(ring1[:, ahead % RING1, :, :],
                                     aT_v[ds(jc, 1), :, ahead * GRP1:(ahead + 1) * GRP1, :].rearrange("o p t j -> (o p) t j"))\
                          .then_inc(a1_in[ahead % RING1], 16)
                    else:
                        ahead -= NG1
                        sp.dma_start(ring1[:, ahead % RING1, :, :],
                                     aT_v[ds(jc + 1, 1), :, ahead * GRP1:(ahead + 1) * GRP1, :].rearrange("o p t j -> (o p) t j"))\
                          .then_inc(a1_in[ahead % RING1], 16)

            with sp.Fori(0, NC - 1) as jc:
                steady(jc, NG1)
            steady(NC - 1, NG1 - RING1)

            sp.wait_ge(hT_stored, 16 + 16 * NC)
            sp.wait_ge(u_ready, NC)
            sp.wait_ge(code_ready, 2 + NG1 * NC)
            for dst, name in ((wih[:, 0], "edge_WihT"), (wih[:, 1], "node_WihT"), (whh[:, 0], "edge_WhhT"),
                              (whh[:, 1], "node_WhhT"), (gatw, "gat_W"), (bias, "bias")):
                sp.dma_start(dst, ins[name]).then_inc(late_in, 16)
            def load4(c, g, slot):
                src = aT_v[c, :, g * GRP:(g + 1) * GRP, :] if isinstance(c, int) else \
                    aT_v[ds(c, 1), :, g * GRP:(g + 1) * GRP, :].rearrange("o p t j -> (o p) t j")
                sp.dma_start(a4[:, slot, :, :], src).then_inc(a4_in[slot], 16)

            sp.wait_ge(flags_ready, 1)
            wide = sp.value_load(is_wide, min_val=0, max_val=1)
            h_src = h_dram[:, :, :].rearrange("c p j -> p c j")
            h_dst = h.rearrange("p (c q) d -> p c (q d)", c=NC)
            with sp.If(wide > 0):
                sp.wait_ge(wide_done, 1)
                sp.dma_start(ngB[:, 0:HEADS, :], guard_dram[:, 0:CH].partition_broadcast(P)).then_inc(ng0_in, 16)
                sp.wait_ge(ng0_in, 16)
                sp.sem_inc(ng0_ready, HEADS)
                for g in range(RING):
                    load4(0, g, g)
                sp.dma_start(h_dst, h_src).then_inc(h_in, 16)
            with sp.Else():
                for g in range(RING):
                    sp.wait_ge(mask_ready, NT + -(-(g + 1) * GRP * CH * 4 // N))
                    load4(0, g, g)
                sp.wait_ge(mask_ready, NT + -(-(RING * GRP * CH * 4 + NT * P * 4) // N))
                sp.dma_start(h_dst, h_src).then_inc(h_in, 16)

            def load_rows(c, par):
                for src, dst in ((guard_dram, ngB), (rden_dram, rdB)):
                    where = slice(c * CH, (c + 1) * CH) if isinstance(c, int) else ds(c * CH, CH)
                    at = slice(par * HEADS, (par + 1) * HEADS) if isinstance(par, int) else ds(par * HEADS, HEADS)
                    sp.dma_start(dst[:, at, :], src[:, where].partition_broadcast(P)).then_inc(rows_in, 16)

            def store_rows():
                sp.wait_ge(rows_ready, 1)
                with sp.If(wide > 0):
                    sp.sem_inc(sp_idle, 1)
                with sp.Else():
                    for s, dst in enumerate((guard_dram, rden_dram)):
                        sp.dma_start(dst[:, :].rearrange("k (t p) -> t k p", p=P), rows[:, s, :]).then_inc(guard_stored, 16)
                    sp.wait_ge(guard_stored, 32)
                sp.dma_start(rdB[:, 0:HEADS, :], rden_dram[:, 0:CH].partition_broadcast(P)).then_inc(rows_in, 16)

            def chunk_loads(c, groups, first=False, last=False):
                for g in groups:
                    if g == 4 and not last:
                        if first:
                            store_rows()
                        else:
                            sp.wait_ge(nn_taken, c * HEADS)
                        load_rows(c + 1, (c + 1) % 2)
                    if g == 6:
                        if not first:
                            sp.wait_ge(yT_done, c)
                        sp.dma_start(hTc, hT_dram[ds(c, 1), :, :].rearrange("o p j -> (o p) j")).then_inc(hT_in, 16)
                    if last and g >= NG - RING:
                        continue
                    sp.wait_ge(tile_done, c * NT + (4 + GRP * (g + 1)))
                    if g + RING < NG:
                        load4(c, g + RING, g % RING)
                    else:
                        load4(c + 1, g + RING - NG, g % RING)

            chunk_loads(0, range(NG), first=True)
            with sp.Fori(1, NC - 1) as c:
                chunk_loads(c, range(NG))
            chunk_loads(NC - 1, range(NG), last=True)

        @block.tensor
        def _(pe):
            pe.wait_ge(const_ready, 2)
            pe.wait_ge(w0_in, 16)

            def transpose_x(i):
                for b in range(2):
                    pe.wait_ge(g0_ready, 2 * i + b + 1)
                    for q in range(QT):
                        last = nc.tensor.transpose(bank[4 + b][:, q * P:(q + 1) * P], gx[:, b * QT + q, :], ident[:, :])
                    last.then_inc(g0T_done, 1)

            def support(i):
                for b in range(2):
                    pe.wait_ge(g0T_ready, 2 * i + b + 1)
                    for q in range(QT):
                        last = nc.tensor.matmul(bank[2 + b][:, q * P:(q + 1) * P], gT[:, b, q * P:(q + 1) * P], w0[:, :],
                                                start=True, stop=True)
                    last.then_inc(S_done, 1)

            def products(jc, groups, into):
                for g in groups:
                    pe.wait_ge(a1_in[g % RING1], jc * (16 * NG1 // RING1) + 16 * (g // RING1 + 1))
                    for r in range(GRP1):
                        it = g * GRP1 + r
                        last = nc.tensor.matmul(bank[into][:, :], S[:, it, :], ring1[:, g % RING1, r, :],
                                                start=(it == 0), stop=(it == NT - 1))
                    last.then_inc(a1_used_pe, 1)

            def to_natural(done):
                pe.wait_ge(oT_ready, done)
                for q in range(QT):
                    last = nc.tensor.transpose(bank[1][:, q * P:(q + 1) * P], oT[:, q * P:(q + 1) * P], ident[:, :])
                last.then_inc(o_nat, 1)

            def transpose_h(done):
                pe.wait_ge(h_ready, done)
                for q in range(QT):
                    last = nc.tensor.transpose(bank[2][:, q * P:(q + 1) * P], gx[:, q, :], ident[:, :])
                last.then_inc(hT_done, 1)

            def project(done):
                pe.wait_ge(hT_ready, done)
                for q in range(QT):
                    last = nc.tensor.matmul(bank[3][:, q * 8:q * 8 + 6], gT[:, 0, q * P:(q + 1) * P], V[:, :],
                                            start=True, stop=True)
                last.then_inc(u_done, 1)

            transpose_x(0)
            support(0)
            for i in range(ROUNDS):
                pe.wait_ge(S_ready, 2 * (i + 1))
                products(0, range(i * RG, i * RG + RG // 2), OUT[0])
                if i + 1 < ROUNDS:
                    transpose_x(i + 1)
                products(0, range(i * RG + RG // 2, (i + 1) * RG), OUT[0])
                if i + 1 < ROUNDS:
                    support(i + 1)
            pe.wait_ge(consts_in, 48)
            for s in range(2):
                for k in range(HEADS):
                    c = s * HEADS + k
                    last = nc.tensor.matmul(bank[7][:, c:c + 1], wT[:, k, :], av[:, c:c + 1], start=True, stop=True)
            last.then_inc(v_done, 1)

            pe.wait_ge(v_ready, 1)
            def chunk1(jc, into):
                products(jc, range(0, 2), into)
                to_natural(jc)
                products(jc, range(2, 8), into)
                transpose_h(jc)
                products(jc, range(8, 12), into)
                project(jc)
                products(jc, range(12, NG1), into)

            with pe.Fori(0, NC // 2 - 1) as m:
                chunk1(m * 2 + 1, OUT[1])
                chunk1(m * 2 + 2, OUT[0])
            chunk1(NC - 1, OUT[1])
            to_natural(NC)
            transpose_h(NC)
            project(NC)

            def mask_products(moving, cols, turn0, sides):
                depth = MASKS // sides
                with pe.Fori(0, NT // depth) as i:
                    for b in range(depth):
                        n = i * depth + (turn0 + b)
                        pe.wait_ge(mask_ready, n + 1)
                        pe.wait_ge(sums_taken, n + (MASKS + 1 - depth))
                        pe.sem_inc(pe_idle, 1)
                        for s in range(sides):
                            for it in range(NT):
                                last = nc.tensor.matmul(bank[b][:, 0:cols], masks[:, b * sides + s, it, :],
                                                        moving[:, s, it, :], start=(s == 0 and it == 0),
                                                        stop=(s == sides - 1 and it == NT - 1))
                        last.then_inc(mask_used, 1)

            pe.wait_ge(neg_known, 1)
            negatives = pe.value_load(any_neg, min_val=0, max_val=1)
            with pe.If(negatives > 0):
                pe.wait_ge(u_pos_ready, 1)
                pe.wait_ge(u_neg_ready, 1)
                mask_products(mvU, 21, 0, 2)
            with pe.Else():
                pe.wait_ge(u_pos_ready, 1)
                mask_products(mvU, 21, 0, 1)
            with pe.If(negatives > 0):
                pe.wait_ge(w_pos_ready, 1)
                pe.wait_ge(w_neg_ready, 1)
                mask_products(mvW, KG * 3, NT, 2)
            with pe.Else():
                pe.wait_ge(w_pos_ready, 1)
                mask_products(mvW, KG * 3, NT, 1)

            def a4_support(c, it):
                g, r = it // GRP, it % GRP
                if r == 0:
                    pe.wait_ge(a4_clean, c * NG + (g + 1))
                if it == 0 and not (isinstance(c, int) and c == 0):
                    pe.wait_ge(sup_taken, c)
                nc.tensor.matmul(bank[3][:, :], h[:, it, :], a4[:, g % RING, r, :], start=(it == 0), stop=(it == NT - 1))

            def tile(c, it):
                first = isinstance(c, int) and c == 0
                if not first:
                    a4_support(c, it)
                elif it + AHEAD < NT:
                    a4_support(c, it + AHEAD)
                for k in range(HEADS):
                    pe.wait_ge(w_ready, c * (NT * HEADS) + (6 + it * HEADS + k + 1))
                    if it == 0 and not first:
                        pe.wait_ge(nn_taken, c * HEADS + (k + 1 - HEADS))
                    last = nc.tensor.matmul(bank[k][:, :], h[:, it, :], wgt[:, it % RING, k, :],
                                            start=(it == 0), stop=(it == NT - 1))
                last.then_inc(tile_done, 1)

            def spread_guards():
                for k in range(HEADS):
                    pe.wait_ge(gdiag_ready, k + 1)
                    nc.tensor.matmul(bank[4 + k][:, :], all_ones, gdiag[k], start=True, stop=True).then_inc(g_spread, 1)

            def guards_to_rows():
                pe.wait_ge(nat_ready, 1)
                nc.tensor.transpose(bank[7][0:HEADS * NT, 0:P], nguard, ident[:, :])
                nc.tensor.transpose(bank[7][0:HEADS * NT, P:2 * P], rden, ident[:, :]).then_inc(rows_done, 1)

            pe.wait_ge(flags_ready, 1)
            wide = pe.value_load(is_wide, min_val=0, max_val=1)
            with pe.If(wide > 0):
                spread_guards()
                with pe.Fori(0, NC) as c:
                    pe.wait_ge(wide_sum, c + 1)
                    for k in range(HEADS):
                        last = nc.tensor.matmul(bank[k][:, :], all_ones, wide_acc[:, k * CH:(k + 1) * CH],
                                                start=True, stop=True)
                    last.then_inc(wide_total, 1)
                pe.wait_ge(h_in, 16)
                for it in range(AHEAD):
                    a4_support(0, it)
            with pe.Else():
                pe.wait_ge(h_in, 16)
                pe.wait_ge(sums_taken, MASKS + 2 * NT)
                for it in range(AHEAD - 3):
                    a4_support(0, it)
                spread_guards()
                for it in range(AHEAD - 3, AHEAD):
                    a4_support(0, it)

            def hidden(cell, banks=(4, 5, 6, 7)):
                for gate, b in enumerate((banks[1], banks[2], banks[0])):
                    nc.tensor.matmul(bank[b][:, :], whh[:, cell, gate, :], hTc, start=True, stop=(gate == 2))

            def after(e, it, last_chunk=False):
                if it == "start":
                    pe.wait_ge(hT_in, e * 16)
                    hidden(0)
                if it == 1:
                    pe.wait_ge(nn_taken, e * HEADS)
                    for k in range(HEADS):
                        last = nc.tensor.matmul(bank[7][:, :], gatw[:, k, :], nn[k], start=(k == 0), stop=(k == HEADS - 1))
                    last.then_inc(es_done, 1)
                if it == 3:
                    pe.wait_ge(sup_taken, e)
                    for b, gate in ((5, 0), (6, 1)):
                        last = nc.tensor.matmul(bank[b][:, :], wih[:, 0, gate, :], sup, start=False, stop=True)
                    last.then_inc(gate_done, 1)
                if it == 5:
                    pe.wait_ge(es_ready, e)
                    nc.tensor.matmul(bank[7][:, :], wih[:, 0, 2, :], sup, start=True, stop=True).then_inc(ni_done, 1)
                if it == 12:
                    banks = cell_banks(1, last_chunk)
                    if not last_chunk:
                        pe.wait_ge(cand_ready, e * 2 - 1)
                    hidden(1, banks)
                    for gate in range(2):
                        last = nc.tensor.matmul(bank[banks[1 + gate]][:, :], wih[:, 1, gate, :], es, start=False, stop=True)
                    last.then_inc(gate_done, 1)
                    nc.tensor.matmul(bank[banks[3]][:, :], wih[:, 1, 2, :], es, start=True, stop=True).then_inc(ni_done, 1)
                if it == 23:
                    y = cell_buffers(1, last_chunk)[1]
                    pe.wait_ge(ysum_ready, e)
                    for q in range(QT):
                        last = nc.tensor.transpose(bank[4][:, q * P:(q + 1) * P], y[:, q * P:(q + 1) * P], ident[:, :])
                    last.then_inc(yT_done, 1)

            pe.wait_ge(late_in, 96)
            for it in range(NT):
                tile(0, it)
                if it == DEN_AT + 3:
                    guards_to_rows()
            with pe.Fori(1, NC) as c:
                after(c, "start")
                for it in range(NT):
                    tile(c, it)
                    after(c, it)
            for it in ["start", *range(NT)]:
                after(NC, it, last_chunk=True)

        @block.scalar
        def _(act):
            def signs(jc, groups):
                for g in groups:
                    act.wait_ge(a1_in[g % RING1], jc * (16 * NG1 // RING1) + 16 * (g // RING1 + 1))
                    act.wait_ge(code_ready, jc * NG1 + (g + 1))
                    nc.scalar.activation(sgn[:, g % 2, :], ring1[:, g % RING1, :, :], ACT.Sign).then_inc(a1_used_act, 1)

            def take_out(done, out_of):
                act.wait_ge(a1_used_pe, done * NG1)
                nc.scalar.activation(oT[:, :], bank[out_of][:, :], ACT.Relu, bias=b0[:, 0:1]).then_inc(oT_ready, 1)

            def root(done):
                act.wait_ge(var_ready, done)
                nc.scalar.activation(sq[:, 0:QT], sd[:, 0:QT], ACT.Sqrt).then_inc(sqrt_ready, 1)

            def take_hT(done):
                act.wait_ge(hT_done, done)
                act.wait_ge(hT_stored, done * 16)
                nc.scalar.copy(gT[:, 0, :], bank[2][:, :]).then_inc(hT_ready, 1)
                act.wait_ge(h_ready, done)
                act.dma_start(h_dram[ds(done - 1, 1), :, :].rearrange("o p j -> (o p) j"),
                              gx[:, 0:QT, :].rearrange("p q d -> p (q d)")).then_inc(h_stored, 16)
                act.wait_ge(hT_ready, done)
                act.dma_start(hT_dram[ds(done - 1, 1), :, :].rearrange("o p j -> (o p) j"), gT[:, 0, :]).then_inc(hT_stored, 16)

            def roots(i):
                act.wait_ge(var_ready, i + 1)
                at = slice(i * RT, (i + 1) * RT)
                nc.scalar.activation(sq[:, at], sd[:, at], ACT.Sqrt).then_inc(sqrt_ready, 1)

            def take_gT(i):
                for b in range(2):
                    act.wait_ge(g0T_done, 2 * i + b + 1)
                    nc.scalar.copy(gT[:, b, :], bank[4 + b][:, :]).then_inc(g0T_ready, 1)

            def take_S(i):
                for b in range(2):
                    act.wait_ge(S_done, 2 * i + b + 1)
                    at = (2 * i + b) * QT
                    nc.scalar.copy(S[:, at:at + QT, :], bank[2 + b][:, :].rearrange("p (q d) -> p q d", q=QT))\
                      .then_inc(S_ready, 1)

            act.wait_ge(const_ready, 1)
            nc.scalar.activation(tops[:, 84:85], ident[:, 0:1], ACT.Sqrt, scale=0.0)
            roots(0)
            roots(1)
            take_gT(0)
            take_S(0)
            roots(2)
            signs(0, range(0, 2))
            roots(3)
            take_gT(1)
            signs(0, range(2, 4))
            take_S(1)
            signs(0, range(4, 6))
            take_gT(2)
            signs(0, range(6, 8))
            take_S(2)
            signs(0, range(8, 10))
            take_gT(3)
            signs(0, range(10, 12))
            take_S(3)
            signs(0, range(12, NG1))
            act.wait_ge(v_done, 1)
            nc.scalar.copy(V[:, :], bank[7][:, 0:6]).then_inc(v_ready, 1)

            def chunk1(jc, before):
                take_out(jc, before)
                signs(jc, range(0, 5))
                root(jc + ROUNDS)
                signs(jc, range(5, 10))
                take_hT(jc)
                signs(jc, range(10, NG1))

            with act.Fori(0, NC // 2 - 1) as m:
                chunk1(m * 2 + 1, OUT[0])
                chunk1(m * 2 + 2, OUT[1])
            chunk1(NC - 1, OUT[0])
            take_out(NC, OUT[1])
            root(NC + ROUNDS)
            take_hT(NC)
            act.wait_ge(h_stored, 16 + 16 * NC)
            nc.scalar.activation(tops[:, 84:85], b0[:, 0:1], ACT.Exp, scale=0.0)
            act.wait_ge(neg_known, 1)
            negatives = act.value_load(any_neg, min_val=0, max_val=1)
            act.wait_ge(arg_ready, 1)
            nc.scalar.activation(ww, t2, ACT.Exp).then_inc(exp_ready, 1)
            with act.If(negatives > 0):
                act.wait_ge(arg_neg_ready, 1)
                nc.scalar.activation(ww, t2, ACT.Exp).then_inc(exp_neg_ready, 1)
            with act.Else():
                act.sem_inc(act_idle, 1)
            act.wait_ge(flags_ready, 1)
            wide = act.value_load(is_wide, min_val=0, max_val=1)
            with act.If(wide > 0):
                with act.Fori(0, NC) as c:
                    for it in range(NT):
                        for s in range(2):
                            for k in range(HEADS):
                                at = slice(k * CH, (k + 1) * CH)
                                act.wait_ge(wide_arg, c * (NT * 2 * HEADS) + ((it * 2 + s) * HEADS + k + 1))
                                nc.scalar.activation(wide_expo[:, at], wide_args[:, at], ACT.Exp,
                                                     bias=scores[:, it, s * HEADS + k:s * HEADS + k + 1]).then_inc(wide_exp, 1)
                    act.wait_ge(wide_rows, c + 1)
                    for k in range(HEADS):
                        at = slice(k * CH, (k + 1) * CH)
                        act.dma_start(guard_dram[k:k + 1, ds(c * CH, CH)], wide_ng[0:1, at]).then_inc(wide_stored, 16)
                        act.dma_start(rden_dram[k:k + 1, ds(c * CH, CH)], wide_args[0:1, at]).then_inc(wide_stored, 16)
                act.wait_ge(wide_stored, 32 * HEADS * NC)
                act.sem_inc(wide_done, 1)
            with act.Else():
                for k in range(HEADS):
                    act.wait_ge(g_spread, k + 1)
                    nc.scalar.copy(ngB[:, k, :], bank[4 + k][:, :]).then_inc(ng0_ready, 1)

            def exponentials(c, it):
                for k in range(HEADS):
                    n = c * (NT * HEADS) + (it * HEADS + k + 1)
                    act.wait_ge(arg4_ready, n)
                    act.wait_ge(w_ready, n)
                    nc.scalar.activation(expo[:, it % 2, k, :], args[:, it % 2, k, :], ACT.Exp,
                                         bias=scores[:, it, k:k + 1]).then_inc(e_ready, 1)

            def after(e, it, last_chunk=False):
                if it == 1:
                    act.wait_ge(tile_done, e * NT + 4)
                    nc.scalar.copy(sup, bank[3][:, :]).then_inc(sup_taken, 1)
                if it == 4:
                    act.wait_ge(es_done, e)
                    nc.scalar.copy(es, bank[7][:, :]).then_inc(es_ready, 1)
                for cell, at in ((0, 6), (1, 14)):
                    n = e * 2 - (1 - cell)
                    banks = cell_banks(cell, last_chunk)
                    arg, _, r, z, candidate = cell_buffers(cell, last_chunk)
                    if it == at:
                        act.wait_ge(gate_done, n)
                        if cell == 1 and not last_chunk:
                            act.wait_ge(y_ready, n - 1)
                        nc.scalar.activation(r, bank[banks[1]][:, :], ACT.Tanh, scale=0.5, bias=hbias[:, 2 * cell:2 * cell + 1])\
                          .then_inc(act_gate, 1)
                        nc.scalar.activation(z, bank[banks[2]][:, :], ACT.Tanh, scale=0.5, bias=hbias[:, 2 * cell + 1:2 * cell + 2])\
                          .then_inc(act_gate, 1)
                    if it == at + 3:
                        act.wait_ge(pre_ready, n)
                        nc.scalar.activation(candidate, arg, ACT.Tanh, bias=bias[:, 6 * cell + 2:6 * cell + 3])\
                          .then_inc(cand_ready, 1)
                if it == 28:
                    act.wait_ge(ot_ready, e)
                    act.dma_start(out_v[ds(e - 1, 1)].rearrange("o p q d -> (o p) q d"), ot.rearrange("p (q d) -> p q d", q=QT))\
                       .then_inc(out_stored, 16)

            def act_chunk(c, e=None):
                for it in range(NT):
                    exponentials(c, it)
                    if e is not None:
                        after(e, it)
                    elif it == DEN_AT + 1:
                        act.wait_ge(arg_ready, 2)
                        nc.scalar.activation(ww, tt, ACT.Exp).then_inc(exp_ready, 1)

            act.wait_ge(hb_ready, 1)
            act_chunk(0)
            with act.Fori(1, NC) as c:
                act_chunk(c, c)
            for it in range(NT):
                after(NC, it, last_chunk=True)
            act.wait_ge(out_stored, 16 + 16 * NC)

        @block.vector
        def _(dve):
            own, no = Chain(dve, dve_own, dve_idle), Chain(dve, neg_own, dve_idle)
            dve.sem_inc(code_ready, 2)
            own.step(nc.vector.memset(any_bits, 0))

            def stats_of_x(i):
                if i > 0:
                    dve.wait_ge(xin_done[i], 16)
                for t in range(i * RT, (i + 1) * RT):
                    if t in (0, QT):
                        dve.wait_ge(x0_in[t // QT], 16)
                    own.step(nc.vector.bn_stats(stats[:, t, :], x1[:, t, :]), wait=(t == (i + 1) * RT - 1))
                for t in range(i * RT, (i + 1) * RT):
                    own.step(nc.vector.bn_aggr(mv[:, t, :], stats[:, t, :]), wait=(t == (i + 1) * RT - 1))
                variance(i * RT, RT)

            def variance(at, n):
                nc.vector.tensor_scalar(sd[:, at:at + n], mv[:, at:at + n, 1], EPS, None, ALU.add).then_inc(var_ready, 1)

            def inverse_root(at, n):
                root, inv, var = sq[:, at:at + n], rstd[:, at:at + n], sd[:, at:at + n]
                own.step(nc.vector.reciprocal(inv, root))
                own.step(nc.vector.tensor_tensor(inv, inv, var, ALU.mult))
                own.step(nc.vector.tensor_tensor(root, inv, root, ALU.add))
                own.step(nc.vector.tensor_scalar(root, root, 0.5, None, ALU.mult))
                own.step(nc.vector.reciprocal(inv, root))

            def ln_relu(dst0, src, mean, scale):
                for q in range(QT):
                    own.step(nc.vector.tensor_scalar(gx[:, dst0 + q, :], src(q), mean(q), scale(q),
                                                     ALU.subtract, ALU.mult), wait=(q == QT - 1))

            def normalise_x(i):
                dve.wait_ge(var_ready, i + 1)
                dve.wait_ge(sqrt_ready, i + 1)
                inverse_root(i * RT, RT)
                for b in range(2):
                    at = i * RT + b * QT
                    if i > 0:
                        dve.wait_ge(g0T_done, 2 * (i - 1) + b + 1)
                    ln_relu(b * QT, lambda q: x1[:, at + q, :], lambda q: mv[:, at + q, 0:1],
                            lambda q: rstd[:, at + q:at + q + 1])
                    nc.vector.tensor_scalar(gx[:, b * QT:(b + 1) * QT, :], gx[:, b * QT:(b + 1) * QT, :], 0.0, None, ALU.max)\
                      .then_inc(g0_ready, 1)

            def codes(jc, groups):
                for g in groups:
                    dve.wait_ge(a1_used_act, jc * NG1 + (g + 1))
                    nc.vector.tensor_scalar(
                        codes8[:, ds(jc * QT, QT), g * GRP1:(g + 1) * GRP1, :].rearrange("p n t j -> p t n j"),
                        sgn[:, g % 2, :].rearrange("p (t n j) -> p t n j", t=GRP1, n=QT), CODE_STEP, CODE_ZERO,
                        ALU.mult, ALU.add).then_inc(code_ready, 1)
                    dve.wait_ge(code_ready, jc * NG1 + (g + 3))
                    own.step(nc.vector.tensor_tensor(any_bits, any_bits, code32[:, ds(jc * QT, QT), g * GRP1:(g + 1) * GRP1, :],
                                                     ALU.bitwise_or), wait=False)

            def residual(done):
                dve.wait_ge(o_nat, done)
                c = x1[:, ds(done * QT - QT, QT), :]
                own.step(nc.vector.tensor_tensor(c, c, bank[1][:, :].rearrange("p (q d) -> p q d", q=QT), ALU.add))
                own.stand()
                for q in range(QT):
                    own.step(nc.vector.bn_stats(stats[:, q, :], x1[:, ds(done * QT - QT + q, 1), :]), wait=(q == QT - 1))
                own.stand()
                for q in range(QT):
                    own.step(nc.vector.bn_aggr(mv[:, q, :], stats[:, q, :]), wait=(q == QT - 1))
                variance(0, QT)

            def normalise(done):
                dve.wait_ge(var_ready, done + ROUNDS)
                dve.wait_ge(sqrt_ready, done + ROUNDS)
                inverse_root(0, QT)
                dve.wait_ge(h_stored, done * 16)
                ln_relu(0, lambda q: x1[:, ds(done * QT - QT + q, 1), :], lambda q: mv[:, q, 0:1],
                        lambda q: rstd[:, q:q + 1])
                nc.vector.tensor_scalar(gx[:, 0:QT, :], gx[:, 0:QT, :], 0.0, None, ALU.max).then_inc(h_ready, 1)

            def take_u(done):
                dve.wait_ge(u_done, done)
                nc.vector.tensor_copy(u6[:, ds(done * QT - QT, QT), :],
                                      bank[3][:, 0:32].rearrange("p (q s) -> p q s", q=QT)[:, :, 0:6]).then_inc(u_ready, 1)

            stats_of_x(0)
            normalise_x(0)
            stats_of_x(1)
            stats_of_x(2)
            normalise_x(1)
            codes(0, range(0, 2))
            stats_of_x(3)
            normalise_x(2)
            codes(0, range(2, 4))
            normalise_x(3)
            codes(0, range(4, NG1))
            dve.wait_ge(g0T_done, NC)
            base = own.at
            with dve.Fori(1, NC) as jc:
                own.at = jc * OWN1 + (base - OWN1)
                codes(jc, range(0, 4))
                residual(jc)
                codes(jc, range(4, 6))
                normalise(jc)
                codes(jc, range(6, 13))
                take_u(jc)
                codes(jc, range(13, NG1))
            own.at = base + OWN1 * (NC - 1)
            dve.wait_ge(dve_own, own.at)
            no.step(nc.vector.tensor_scalar(bits_flat.bitcast(U32), bits_flat.bitcast(U32), NEG_BITS, None, ALU.bitwise_and))
            no.step(nc.vector.tensor_copy(t2[:, 256:512], bits_flat.bitcast(I32)))
            no.step(nc.vector.tensor_reduce(tops[:, 80:81], t2[:, 256:512], AX.X, ALU.max))
            nc.vector.tensor_scalar(tops[:, 80:81], tops[:, 80:81], 1.0, None, ALU.min).then_inc(neg_found, 1)
            residual(NC)
            dve.wait_ge(neg_reduced, 1)
            nc.vector.tensor_copy(tops[:, 82:83].bitcast(I32), tops[:, 81:82]).then_inc(neg_known, 1)
            normalise(NC)
            dve.wait_ge(neg_known, 1)
            negatives = dve.value_load(any_neg, min_val=0, max_val=1)

            dve.wait_ge(code_ready, 2 + NG1 * NC)
            diag = big[:, :].bitcast(U32).rearrange("p (b j) -> p b j", j=P // 4)[:, ::NT + 1, :]
            own.step(nc.vector.tensor_tensor(diag, diag, notI[:, :].bitcast(U32)[:, None, :].to_broadcast([P, NT, P // 4]),
                                             ALU.bitwise_and), wait=False)

            depth_of = lambda sides: MASKS // sides

            def make_masks(n, b, turn0, sides):
                dve.wait_ge(mask_used, n + (turn0 + MASKS + 1 - depth_of(sides)))
                for s, bits in enumerate((POS_BITS, NEG_BITS)[:sides]):
                    last = nc.vector.tensor_scalar(masks32[:, b * sides + s, :, :],
                                                   code32[:, ds(n, 1), :, :].rearrange("p o t j -> p (o t) j"),
                                                   bits, None, ALU.bitwise_and)
                last.then_inc(mask_ready, 1)

            def masks_ahead(turn0, some):
                with dve.If(negatives > 0):
                    dve.sem_inc(dve_idle, 1)
                    for n in some:
                        if n < depth_of(2) - 1:
                            make_masks(n, n, turn0, 2)
                with dve.Else():
                    for n in some:
                        make_masks(n, n, turn0, 1)

            def mask_sums(turn0, cols, dst):
                def turns(sides):
                    depth = depth_of(sides)
                    ahead = depth - 1

                    def take(n, b):
                        dve.wait_ge(mask_used, n + (turn0 + MASKS + 1))
                        nc.vector.tensor_reduce(dst[:, ds(n, 1), :], bank[b][:, 0:cols].rearrange("p (c r) -> p c r", r=3),
                                                AX.X, ALU.add).then_inc(sums_taken, 1)

                    with dve.Fori(0, NT // depth - 1) as i:
                        for b in range(depth):
                            make_masks(i * depth + (b + ahead), (b + ahead) % depth, turn0, sides)
                            take(i * depth + b, b)
                    make_masks(NT - 1, depth - 1, turn0, sides)
                    for b in range(depth):
                        take(NT - depth + b, b)

                with dve.If(negatives > 0):
                    turns(2)
                with dve.Else():
                    turns(1)
                dve.wait_ge(sums_taken, turn0 + MASKS + NT)

            own.step(nc.vector.memset(all_ones, 1.0), wait=False)
            for g in range(WIN):
                own.step(nc.vector.memset(below[:, g:g + 1], 1.0 - WIDTH / 2 - WIDTH * g), wait=False)
            own.step(nc.vector.memset(mvU[:, 0, :, 18:21], 0.0), wait=False)
            own.step(nc.vector.memset(mvU[:, 1, :, 19:21], 0.0), wait=False)
            own.step(nc.vector.memset(mvU[:, 1, :, 18:19], 1 / NEG_VALUE), wait=False)
            dve.wait_ge(dve_own, own.at)
            dve.wait_ge(a1_used_pe, NG1 * NC)
            masks_ahead(0, range(2))
            take_u(NC)

            def pieces(value, piece, rest, ready):
                own.step(nc.vector.tensor_copy(piece(0), value))
                own.step(nc.vector.tensor_tensor(rest, value, piece(0), ALU.subtract))
                own.step(nc.vector.tensor_copy(piece(1), rest))
                nc.vector.tensor_tensor(piece(2), rest, piece(1), ALU.subtract).then_inc(ready, 1)

            dve.wait_ge(u_ready, NC)
            flat = lambda a: a.rearrange("p t s -> p (t s)")
            own.step(nc.vector.tensor_scalar(mm[:, 0:NT * 6], flat(u6), 1 / POS_VALUE, None, ALU.mult))
            mvU5 = mvU[:, :, :, :].rearrange("p s t (c r) -> p s t c r", r=3)
            split = lambda a: a.rearrange("p (t c) -> p t c", t=NT)
            pieces(split(mm[:, 0:NT * 6]), lambda r: mvU5[:, 0, :, 0:6, r], split(tt[:, 0:NT * 6]),
                   u_pos_ready)
            dve.wait_ge(u_pos_ready, 1)
            own.step(nc.vector.tensor_scalar(mvU[:, 1, :, 0:9], mvU[:, 0, :, 9:18], POS_VALUE / NEG_VALUE, None, ALU.mult), wait=False)
            nc.vector.tensor_scalar(mvU[:, 1, :, 9:18], mvU[:, 0, :, 0:9], POS_VALUE / NEG_VALUE, None, ALU.mult)\
              .then_inc(u_neg_ready, 1)

            masks_ahead(0, range(2, MASKS - 1))
            mask_sums(0, 21, scores)
            own.step(nc.vector.scalar_tensor_tensor(flat(scores), flat(scores), ALPHA, flat(scores), ALU.mult, ALU.max))
            pos, neg = scores[:, :, 0:HEADS], scores[:, :, HEADS:2 * HEADS]

            both = scores[:, :, 0:2 * HEADS].rearrange("p t k -> p k t")
            own.step(nc.vector.tensor_reduce(tops[:, 0:6], both, AX.X, ALU.max), wait=False)
            own.step(nc.vector.tensor_reduce(tops[:, 6:12], both, AX.X, ALU.min, negate=True), wait=False)
            nc.vector.tensor_reduce(tops[:, 12:13], scores[:, :, 6:7].rearrange("p t k -> p k t"), AX.X, ALU.max)\
              .then_inc(ext_ready, 1)
            masks_ahead(NT, range(1))
            dve.wait_ge(all_ext, 1)
            own.step(nc.vector.tensor_scalar(tops[:, 29:30], tops[:, 28:29], 1.0, None, ALU.min))
            own.step(nc.vector.tensor_scalar(tops[:, 29:30], tops[:, 29:30], 1.0, HUGE, ALU.subtract, ALU.mult))
            for at in (16, 22):
                own.step(nc.vector.tensor_scalar(tops[:, at + 3:at + 6], tops[:, at + 3:at + 6], tops[:, 29:30], None, ALU.add), wait=False)
            dve.wait_ge(dve_own, own.at)
            for at in (16, 22):
                own.step(nc.vector.tensor_tensor(tops[:, at:at + 3], tops[:, at:at + 3], tops[:, at + 3:at + 6], ALU.max), wait=False)
            dve.wait_ge(dve_own, own.at)
            own.step(nc.vector.tensor_copy(tops[:, 32:35].bitcast(I32), tops[:, 16:19]))
            own.step(nc.vector.tensor_copy(tops[:, 36:39], tops[:, 32:35].bitcast(I32)))
            bg = tops[:, 40:40 + KG].rearrange("p (k g) -> p k g", k=HEADS)
            own.step(nc.vector.tensor_tensor(bg, below[:, None, :].to_broadcast([P, HEADS, WIN]),
                                             tops[:, 36:39, None].to_broadcast([P, HEADS, WIN]), ALU.add))
            t4 = tt.rearrange("p (t k g) -> p t k g", t=NT, k=HEADS)
            bgb = bg[:, None, :, :].to_broadcast([P, NT, HEADS, WIN])

            def window_weights(s, e, value, asked, given, ready):
                own.step(nc.vector.tensor_tensor(t4, e[:, :, :, None].to_broadcast([P, NT, HEADS, WIN]), bgb, ALU.subtract))
                nc.vector.tensor_scalar(t2, tt, WIDTH / 2, -WIDTH / 2, ALU.min, ALU.max).then_inc(asked, 1)
                own.step(nc.vector.tensor_scalar(mm, tt, -WIDTH / 2, 1 / value, ALU.is_gt, ALU.mult))
                own.step(nc.vector.scalar_tensor_tensor(mm, tt, WIDTH / 2, mm, ALU.is_le, ALU.mult))
                dve.wait_ge(given, 1)
                own.step(nc.vector.tensor_tensor(ww, ww, mm, ALU.mult))
                pieces(ww, lambda r: mvW[:, s, :, :].rearrange("p t (c r) -> p (t c) r", r=3)[:, :, r], ww, ready)

            window_weights(0, pos, POS_VALUE, arg_ready, exp_ready, w_pos_ready)
            at = own.at
            with dve.If(negatives > 0):
                dve.wait_ge(w_pos_ready, 1)
                window_weights(1, neg, NEG_VALUE, arg_neg_ready, exp_neg_ready, w_neg_ready)
            with dve.Else():
                dve.sem_inc(dve_own, own.at - at)
            masks_ahead(NT, range(1, MASKS - 1))
            own.step(nc.vector.tensor_tensor(tops[:, 64:67], tops[:, 16:19], tops[:, 22:25], ALU.add), wait=False)
            own.step(nc.vector.tensor_tensor(tops[:, 67:70], tops[:, 16:19], tops[:, 22:25], ALU.max))
            own.step(nc.vector.tensor_scalar(tops[:, 64:67], tops[:, 64:67], WIN * WIDTH - 4.0, None, ALU.is_gt), wait=False)
            own.step(nc.vector.tensor_scalar(tops[:, 67:70], tops[:, 67:70], COARSE, None, ALU.is_gt))
            own.step(nc.vector.tensor_reduce(tops[:, 70:71], tops[:, 64:70], AX.X, ALU.max), wait=False)
            own.step(nc.vector.tensor_scalar(tops[:, 71:72], tops[:, 28:29], 1.0, None, ALU.min))
            nc.vector.tensor_copy(tops[:, 72:74].bitcast(I32), tops[:, 70:72]).then_inc(flags_ready, 1)
            mask_sums(NT, KG * 3, wsum)

            ws = flat(wsum)
            own.step(nc.vector.tensor_scalar(tt.bitcast(I32), ws.bitcast(I32), 23, None, ALU.logical_shift_right))
            own.step(nc.vector.tensor_copy(mm, tt.bitcast(I32)))
            own.step(nc.vector.tensor_scalar(tt, mm, 0.0, -HUGE, ALU.is_equal, ALU.mult), wait=False)
            own.step(nc.vector.tensor_scalar(mm, mm, LN2, -126 * LN2, ALU.mult, ALU.add))
            own.step(nc.vector.tensor_tensor(tt, tt, mm, ALU.add))
            own.step(nc.vector.tensor_tensor(t4, t4, bgb, ALU.add))
            gd = guard
            rd = rden
            own.step(nc.vector.tensor_reduce(gd, tt.rearrange("p (c g) -> p c g", g=WIN), AX.X, ALU.max))
            ngd = nguard
            own.step(nc.vector.tensor_scalar(ngd, gd, -1.0, None, ALU.mult))
            ng3 = ngd.rearrange("p (t k) -> p t k", t=NT)
            for k in range(HEADS):
                nc.vector.tensor_tensor(gdiag[k].rearrange("p (q j) -> p q j", j=P), ident[:, None, :].to_broadcast([P, QT, P]),
                                        ng3[:, 0:QT, k:k + 1].to_broadcast([P, QT, P]), ALU.mult).then_inc(gdiag_ready, 1)
            dve.wait_ge(flags_ready, 1)
            wide = dve.value_load(is_wide, min_val=0, max_val=1)
            with dve.If(wide > 0):
                wo = Chain(dve, wide_own, dve_idle)
                dve.wait_ge(g_spread, HEADS)
                bound = (caps, rden.rearrange("p (t k) -> p t k", t=NT))
                for b, e in zip(bound, (pos, neg)):
                    wo.step(nc.vector.tensor_scalar(b, e, -1.0, None, ALU.mult), wait=False)
                dve.wait_ge(wide_own, wo.at)
                at0 = wo.at
                head = lambda a, k: a[:, k * CH:(k + 1) * CH]
                with dve.Fori(0, NC) as c:
                    wo.at = c * WIDE_OWN + at0
                    code = lambda it: codes8[:, ds(c * QT, QT), it, :]
                    by_block = lambda a: a.rearrange("p (n j) -> p n j", j=P)
                    wo.step(nc.vector.memset(wide_acc, -HUGE))
                    for it in range(NT):
                        wo.step(nc.vector.tensor_scalar(by_block(not_pos), code(it), POS_CODE, -HUGE, ALU.not_equal, ALU.mult), wait=False)
                        wo.step(nc.vector.tensor_scalar(by_block(not_neg), code(it), NEG_CODE, -HUGE, ALU.not_equal, ALU.mult))
                        for s, no_edge in enumerate((not_pos, not_neg)):
                            for k in range(HEADS):
                                wo.step(nc.vector.scalar_tensor_tensor(
                                    head(wide_acc, k), no_edge, scores[:, it, s * HEADS + k:s * HEADS + k + 1],
                                    head(wide_acc, k), ALU.add, ALU.max), wait=(k == HEADS - 1))
                    dve.sem_inc(wide_max, 1)
                    dve.wait_ge(wide_reduced, c + 1)
                    wo.step(nc.vector.tensor_scalar(wide_ng, wide_ng, -1.0, None, ALU.mult), wait=False)
                    wo.step(nc.vector.memset(wide_acc, 0.0))
                    for it in range(NT):
                        for s in range(2):
                            for k in range(HEADS):
                                nc.vector.tensor_scalar(head(wide_args, k), head(wide_ng, k), bound[s][:, it, k:k + 1], None, ALU.min)\
                                  .then_inc(wide_arg, 1)
                            for k in range(HEADS):
                                dve.wait_ge(wide_exp, c * (NT * 2 * HEADS) + ((it * 2 + s) * HEADS + k + 1))
                                dve.sem_inc(dve_idle, 1)
                                wo.step(nc.vector.scalar_tensor_tensor(by_block(head(wide_expo, k)), code(it), (POS_CODE, NEG_CODE)[s],
                                                                       by_block(head(wide_expo, k)), ALU.is_equal, ALU.mult))
                                wo.step(nc.vector.tensor_tensor(head(wide_acc, k), head(wide_acc, k), head(wide_expo, k), ALU.add))
                    dve.sem_inc(wide_sum, 1)
                    dve.wait_ge(wide_total, c + 1)
                    for k in range(HEADS):
                        wo.step(nc.vector.tensor_scalar(head(wide_args, k), bank[k][:, :], 1e-20, float(HEADS), ALU.max, ALU.mult),
                                wait=(k == HEADS - 1))
                    nc.vector.reciprocal(wide_args, wide_args).then_inc(wide_rows, 1)
                    dve.wait_ge(wide_stored, c * (32 * HEADS) + 32 * HEADS)
            with dve.Else():
                dve.sem_inc(dve_idle, 1)

            dve.wait_ge(late_in, 96)
            own.step(nc.vector.tensor_scalar(cap, tops[:, 70:71], -1.0, 1.0, ALU.mult, ALU.add))
            own.step(nc.vector.tensor_scalar(caps, pos, -1.0, cap, ALU.mult, ALU.add), wait=False)
            b4 = bias.rearrange("p (c s g) -> p c s g", c=2, s=2)
            own.step(nc.vector.tensor_tensor(hbias.rearrange("p (c g) -> p c g", c=2), b4[:, :, 0, 0:2], b4[:, :, 1, 0:2], ALU.add))
            own.step(nc.vector.tensor_scalar(hbias, hbias, 0.5, None, ALU.mult))

            def find_neg(c, g):
                dve.wait_ge(a4_clean, c * NG + (g + 1))
                edges = a4[:, g % RING, :, :].rearrange("p r j -> p (r j)")
                so.step(nc.vector.tensor_scalar(not_neg4, edges, 0.0, -HUGE, ALU.is_ge, ALU.mult), wait=False)
                so.step(nc.vector.tensor_scalar(is_neg4, edges, 0.0, -HUGE, ALU.is_lt, ALU.mult))

            def arguments(c, it, signed):
                edge = slice((it % GRP) * CH, (it % GRP + 1) * CH)
                for k in range(HEADS):
                    dve.wait_ge(e_ready, c * (NT * HEADS) + (it * HEADS + k + 1))
                    arg, row = args[:, it % 2, k, :], guard_row(c, k)
                    if signed:
                        so.step(nc.vector.tensor_scalar(arg, not_neg4[:, edge], neg[:, it, k:k + 1], None, ALU.add))
                        so.step(nc.vector.scalar_tensor_tensor(arg, is_neg4[:, edge], kept[:, it, k:k + 1], arg,
                                                               ALU.add, ALU.max))
                        so.step(nc.vector.tensor_tensor(arg, arg, row, ALU.add))
                        nc.vector.tensor_scalar(arg, arg, cap, None, ALU.min).then_inc(arg4_ready, 1)
                    else:
                        nc.vector.tensor_scalar(arg, row, caps[:, it, k:k + 1], None, ALU.min).then_inc(arg4_ready, 1)

            def guard_row(c, k):
                return ngB[:, k, :] if isinstance(c, int) and c == 0 else \
                    ngB[:, ds((c % 2) * HEADS + k, 1), :].rearrange("p o j -> p (o j)")

            def weights(c, it):
                for k in range(HEADS):
                    dve.wait_ge(e_ready, c * (NT * HEADS) + (6 + it * HEADS + k + 1))
                    if k == 0:
                        dve.wait_ge(tile_done, c * NT + (it + 1))
                        if it % GRP == 0:
                            dve.wait_ge(a4_clean, c * NG + (it // GRP + 1))
                    nc.vector.tensor_tensor(wgt[:, it % RING, k, :], expo[:, it % 2, k, :],
                                            a4[:, (it // GRP) % RING, it % GRP, :], ALU.mult)\
                      .then_inc(w_ready, 1)

            def after(e, it, last_chunk=False):
                if it == 1:
                    dve.wait_ge(tile_done, e * NT + 4)
                    for k in range(HEADS):
                        nc.vector.tensor_tensor(nn[k], bank[k][:, :],
                                                rdB[:, ds(((e - 1) % 2) * HEADS + k, 1), :].rearrange("p o j -> p (o j)"),
                                                ALU.mult).then_inc(nn_taken, 1)
                for cell, at in ((0, 6), (1, 14)):
                    n = e * 2 - (1 - cell)
                    banks = cell_banks(cell, last_chunk)
                    arg, mixed, r, z, candidate = cell_buffers(cell, last_chunk)
                    if it == at:
                        dve.wait_ge(ni_done, n)
                        own.step(nc.vector.tensor_scalar(arg, bank[banks[0]][:, :], bias[:, 6 * cell + 5:6 * cell + 6], 0.5,
                                                         ALU.add, ALU.mult))
                    if it == at + 1:
                        dve.wait_ge(act_gate, n * 2 - 1)
                        own.step(nc.vector.scalar_tensor_tensor(arg, r, 1.0, arg, ALU.add, ALU.mult))
                        nc.vector.tensor_tensor(arg, arg, bank[banks[3]][:, :], ALU.add).then_inc(pre_ready, 1)
                    if it == at + 5:
                        if last_chunk:
                            dve.wait_ge(cand_ready, n)
                            nc.vector.tensor_tensor(mixed, hTc, candidate, ALU.subtract).then_inc(diff_ready, 1)
                        dve.wait_ge(diff_ready, n)
                        dve.wait_ge(act_gate, n * 2)
                        own.step(nc.vector.scalar_tensor_tensor(mixed, z, 1.0, mixed, ALU.add, ALU.mult))
                        nc.vector.scalar_tensor_tensor(mixed if cell else y_edge, mixed, 0.5, candidate, ALU.mult, ALU.add)\
                          .then_inc(y_ready, 1)
                if it == 20 and last_chunk:
                    dve.wait_ge(y_ready, e * 2)
                    nc.vector.tensor_tensor(mixed, mixed, y_edge, ALU.add).then_inc(ysum_ready, 1)
                if it == 26:
                    dve.wait_ge(yT_done, e)
                    dve.wait_ge(out_stored, e * 16)
                    own.stand()
                    for q in range(QT):
                        j = e * QT - (QT - q)
                        ins_ = nc.vector.scalar_tensor_tensor(ot[:, q * P:(q + 1) * P], bank[4][:, q * P:(q + 1) * P],
                                                              dg[:, ds(j, 1)], x1[:, ds(j, 1), :].rearrange("p o d -> p (o d)"),
                                                              ALU.mult, ALU.add)
                    ins_.then_inc(ot_ready, 1)

            def dve_chunk(c, signed, e=None):
                if signed:
                    find_neg(c, 0)
                arguments(c, 0, signed)
                for it in range(NT):
                    if it + 1 < NT:
                        if signed and (it + 1) % GRP == 0:
                            find_neg(c, (it + 1) // GRP)
                        arguments(c, it + 1, signed)
                    weights(c, it)
                    if e is not None:
                        after(e, it)
                    else:
                        denominators(it)

            def denominators(it):
                if it == DEN_AT:
                    gdb = ng3[:, :, :, None].to_broadcast([P, NT, HEADS, WIN])
                    do.step(nc.vector.tensor_tensor(t4, bgb, gdb, ALU.add))
                    nc.vector.tensor_scalar(tt, tt, 80.0, None, ALU.min).then_inc(arg_ready, 1)
                if it == DEN_AT + 2:
                    dve.wait_ge(exp_ready, 2)
                    do.step(nc.vector.tensor_tensor(ww, ww, ws, ALU.mult))
                    do.step(nc.vector.tensor_reduce(rd, ww.rearrange("p (c g) -> p c g", g=WIN), AX.X, ALU.add))
                    do.step(nc.vector.tensor_scalar(rd, rd, 1e-20, float(HEADS), ALU.max, ALU.mult))
                    nc.vector.reciprocal(rd, rd).then_inc(nat_ready, 1)
                if it == DEN_AT + 6:
                    dve.wait_ge(rows_done, 1)
                    nc.vector.tensor_copy(rows[:, :, :], bank[7][0:HEADS * NT, 0:2 * P].rearrange("p (s j) -> p s j", s=2))\
                      .then_inc(rows_ready, 1)

            def all_chunks(signed):
                for k in range(HEADS):
                    dve.wait_ge(ng0_ready, k + 1)
                dve_chunk(0, signed)
                base, so_base = own.at, so.at
                with dve.Fori(1, NC) as c:
                    own.at = c * OWN4 + (base - OWN4)
                    so.at = c * SIGNED_OWN + (so_base - SIGNED_OWN)
                    dve.wait_ge(rows_in, c * 32 + 16)
                    dve_chunk(c, signed, c)
                own.at = base + OWN4 * (NC - 1)
                for it in range(NT):
                    after(NC, it, last_chunk=True)
                assert own.at == base + OWN4 * NC

            so, do = Chain(dve, signed_own, dve_idle), Chain(dve, den_own, dve_idle)
            signed_edges = dve.value_load(is_signed, min_val=0, max_val=1)
            start = own.at
            with dve.If(signed_edges > 0):
                so.step(nc.vector.tensor_copy(kept, pos))
                nc.vector.memset(pos, 0.0).then_inc(hb_ready, 1)
                all_chunks(True)
            own.at = start
            do.at = 0
            with dve.Else():
                dve.sem_inc(hb_ready, 1)
                all_chunks(False)

        @block.gpsimd
        def _(pool):
            nc.gpsimd.memset(ident[:, :], 0.0).then_inc(pool_own, 1)
            pool.wait_ge(pool_own, 1)
            nc.gpsimd.affine_select(out=ident[:, :], in_=ident[:, :], compare_op=ALU.not_equal, fill=1.0, base=0,
                                    pattern=[[-1, P]], channel_multiplier=1).then_inc(const_ready, 1)
            pool.wait_ge(const_ready, 1)
            nc.gpsimd.tensor_scalar(notI[:, :], ident[:, :], -255.0, 255.0, ALU.mult, ALU.add).then_inc(const_ready, 1)
            pool.sem_inc(h_stored, 16)
            pool.sem_inc(hT_stored, 16)
            pool.sem_inc(mask_used, MASKS)
            pool.sem_inc(sums_taken, MASKS)
            pool.sem_inc(tile_done, RING)
            pool.sem_inc(e_ready, 2 * HEADS)
            pool.sem_inc(w_ready, 2 * HEADS)
            pool.sem_inc(out_stored, 16)
            pool.wait_ge(neg_found, 1)
            nc.gpsimd.partition_all_reduce(tops[:, 81:82], tops[:, 80:81], P, RMAX).then_inc(neg_reduced, 1)
            pool.wait_ge(ext_ready, 1)
            nc.gpsimd.partition_all_reduce(tops[:, 16:29], tops[:, 0:13], P, RMAX).then_inc(all_ext, 1)
            pool.wait_ge(u_ready, NC)
            nc.gpsimd.memset(offdiag, 1.0).then_inc(offd_ready, 1)
            pool.wait_ge(offd_ready, 1)
            nc.gpsimd.tensor_scalar(offdiag[:, (NC - 1) * P:NC * P], ident[:, :], -1.0, 1.0, ALU.mult, ALU.add).then_inc(offd_ready, 1)
            pool.wait_ge(offd_ready, 2)
            pool.wait_ge(xdg_in, 16)

            pool.wait_ge(flags_ready, 1)
            wide = pool.value_load(is_wide, min_val=0, max_val=1)
            with pool.If(wide > 0):
                with pool.Fori(0, NC) as c:
                    pool.wait_ge(wide_max, c + 1)
                    pool.sem_inc(pool_idle, 1)
                    nc.gpsimd.partition_all_reduce(wide_ng, wide_acc, P, RMAX).then_inc(wide_reduced, 1)
            with pool.Else():
                pool.sem_inc(pool_idle, 1)

            def clean(c, g):
                pool.wait_ge(a4_in[g % RING], c * (16 * NG // RING) + 16 * (g // RING + 1))
                pool.sem_inc(pool_idle, 1)
                blocks = a4[:, g % RING, :, :].rearrange("p r (b j) -> p (r b) j", j=P)[:, ::QT + 1, :]
                at = (NC - 1 + g - c) * P
                m = offdiag[:, at:at + P] if isinstance(c, int) else offdiag[:, ds(at, P)]
                nc.gpsimd.tensor_tensor(blocks, blocks, m[:, None, :].to_broadcast([P, GRP, P]), ALU.mult).then_inc(a4_clean, 1)

            def after(e, it):
                for cell, at in ((0, 10), (1, 18)):
                    n = e * 2 - (1 - cell)
                    if it == at:
                        pool.wait_ge(cand_ready, n)
                        if cell == 1:
                            pool.wait_ge(y_ready, n - 1)
                        pool.sem_inc(pool_idle, 1)
                        nc.gpsimd.tensor_tensor(mix, hTc, cell_n, ALU.subtract).then_inc(diff_ready, 1)
                if it == 20:
                    pool.wait_ge(y_ready, e * 2)
                    pool.sem_inc(pool_idle, 1)
                    nc.gpsimd.tensor_tensor(mix, mix, y_edge, ALU.add).then_inc(ysum_ready, 1)

            def pool_chunk(c, e=None):
                clean(c, 0)
                clean(c, 1)
                for it in range(NT):
                    if it % GRP == 1 and it // GRP + 2 < NG:
                        clean(c, it // GRP + 2)
                    if e is not None:
                        after(e, it)

            pool_chunk(0)
            with pool.Fori(1, NC) as c:
                pool_chunk(c, c)




def kernel(**inputs):
    import numpy as np
    import concourse.bacc as bacc
    from concourse.bass_utils import run_bass_kernel_spmd

    a = {k: np.asarray(v) for k, v in inputs.items()}
    sent = {
        "x": a["x"],
        "adjT": a["adj"].T.reshape(NT, P, NC, CH).transpose(2, 1, 0, 3),
        "L0_gnn_W": a["L0_gnn_W"],
        "L0_gnn_b": a["L0_gnn_b"],
        "gat_W": a["L1_gnn_gat_W"].transpose(1, 0, 2),
        "gat_WT": a["L1_gnn_gat_W"].transpose(0, 2, 1),
        "gat_a": a["L1_gnn_gat_a"].reshape(HEADS, 2, P).transpose(2, 1, 0).reshape(P, 2 * HEADS),
        "diag": a["adj"].diagonal().reshape(NT, P).T,
        "bias": np.stack([a[f"L1_gnn_{c}_{b}"].reshape(3, P) for c in ("edge", "node") for b in ("bih", "bhh")])
                  .reshape(12, P).T,
        **{f"{c}_{w}T": a[f"L1_gnn_{c}_{w}"].reshape(3, P, P).transpose(2, 0, 1) for c in ("edge", "node") for w in ("Wih", "Whh")},
    }
    nc = bacc.Bacc("TRN2", target_bir_lowering=False, num_devices=1)
    arrays, ins = {}, {}
    for name, value in sent.items():
        arrays[f"in_{name}"] = np.ascontiguousarray(value)
        ins[name] = nc.dram_tensor(f"in_{name}", value.shape, mybir.dt.from_np(value.dtype), kind="ExternalInput").ap()
    out = nc.dram_tensor("out", (N, P), F32, kind="ExternalOutput").ap()
    build(nc, ins, out)
    r = run_bass_kernel_spmd(nc, [arrays], core_ids=[0])
    return r.results[0]["out"]
```
